# Optimizing a Trainium2 kernel written in Bass

```python
import numpy as np
import jax
import jax.numpy as jnp

def _softmax(x, axis=-1):
    return jax.nn.softmax(x, axis=axis)

def _gelu(x):
    return jax.nn.gelu(x, approximate=True)

def _silu(x):
    return jax.nn.silu(x)

def _sigmoid(x):
    return jax.nn.sigmoid(x)

def _layernorm(x, axis=-1, eps=1e-05):
    m = jnp.mean(x, axis=axis, keepdims=True)
    v = jnp.var(x, axis=axis, keepdims=True)
    return (x - m) / jnp.sqrt(v + eps)

def _scatter_add(tgt, idx, src, axis=0):
    return tgt.at[idx].add(src)

def _segment_sum(src, seg, n):
    return jax.ops.segment_sum(src, seg, n)
kernel_name = 'mk_cond_resid_d2_seqx_r2_b13ec0'

def setup_inputs(seed: int=0):
    np.random.seed(seed)
    _w = jnp.asarray

    def _rec_inputs():
        import jax
        import jax.numpy as jnp
        _rk = jax.random.key(seed)
        x = -7.109e-05 + 0.9999 * jax.random.normal(jax.random.fold_in(_rk, 1), (8, 1024, 512), jnp.float32)
        _lenS = 1024 - jax.random.randint(jax.random.fold_in(_rk, 7), (8,), 0, max(1, 1024 // 4) + 1, jnp.int32)
        _lenS2 = 1024 - jax.random.randint(jax.random.fold_in(_rk, 8), (8,), 0, max(1, 1024 // 4) + 1, jnp.int32)
        cond_512 = 0.0061147 + 1.02565 * jax.random.normal(jax.random.fold_in(_rk, 11), (8, 256), jnp.float32)
        return (x, cond_512)
    x, cond_512 = _rec_inputs()

    def _L0_cond_setup():
        import jax, jax.numpy as jnp
        import numpy as np
        W_DIM = 256
        CLAMP = 256.0
        key = jax.random.key(seed)
        ks = jax.random.split(key, 6)
        B, L, C = (8, 4096, 512)
        return {'x': jax.random.normal(ks[0], (B, L, C), dtype=jnp.float32), 'w': jax.random.normal(ks[1], (B, W_DIM), dtype=jnp.float32), 'weight': jax.random.normal(ks[2], (C, C), dtype=jnp.float32), 'bias': jax.random.normal(ks[3], (C,), dtype=jnp.float32), 'affine_w': jax.random.normal(ks[4], (C, W_DIM), dtype=jnp.float32), 'affine_b': jnp.ones((C,), dtype=jnp.float32)}
    _L0_cond_all = _L0_cond_setup()
    _L0_cond_in = {k: v for k, v in _L0_cond_all.items() if k in ('weight', 'bias', 'affine_w', 'affine_b')}
    del _L0_cond_all

    def _L1_cond_setup():
        import jax, jax.numpy as jnp
        import numpy as np
        import math
        HEAD_NUM = 16
        EPS = 1e-08

        def modulated_linear(x, s, aff_w, aff_b, w, b):
            style = s @ aff_w.T + aff_b
            w_mod = w[None, :, :] * style[:, None, :]
            demod = jax.lax.rsqrt(jnp.sum(w_mod * w_mod, axis=2) + EPS)
            w_mod = w_mod * demod[:, :, None]
            return jnp.einsum('bni,boi->bno', x, w_mod) + b
        key = jax.random.key(seed)
        ks = jax.random.split(key, 6)
        B, N, F, S = (8, 512, 512, 256)
        return {'x': jax.random.normal(ks[0], (B, N, F), dtype=jnp.float32), 's': jax.random.normal(ks[1], (B, S), dtype=jnp.float32), 'k_aff_w': jax.random.normal(ks[2], (F, S), dtype=jnp.float32) * 0.02, 'k_aff_b': jnp.ones((F,), dtype=jnp.float32), 'k_w': jax.random.normal(ks[3], (F, F), dtype=jnp.float32) * 0.02, 'k_b': jnp.zeros((F,), dtype=jnp.float32), 'o_aff_w': jax.random.normal(ks[4], (F, S), dtype=jnp.float32) * 0.02, 'o_aff_b': jnp.ones((F,), dtype=jnp.float32), 'o_w': jax.random.normal(ks[5], (F, F), dtype=jnp.float32) * 0.02, 'o_b': jnp.zeros((F,), dtype=jnp.float32)}
    _L1_cond_all = _L1_cond_setup()
    _L1_cond_in = {k: v for k, v in _L1_cond_all.items() if k in ('k_aff_w', 'k_aff_b', 'k_w', 'k_b', 'o_aff_w', 'o_aff_b', 'o_w', 'o_b')}
    del _L1_cond_all
    return {'x': x, 'cond_512': cond_512, 'L0_cond_weight': _L0_cond_in['weight'], 'L0_cond_bias': _L0_cond_in['bias'], 'L0_cond_affine_w': _L0_cond_in['affine_w'], 'L0_cond_affine_b': _L0_cond_in['affine_b'], 'L1_cond_k_aff_w': _L1_cond_in['k_aff_w'], 'L1_cond_k_aff_b': _L1_cond_in['k_aff_b'], 'L1_cond_k_w': _L1_cond_in['k_w'], 'L1_cond_k_b': _L1_cond_in['k_b'], 'L1_cond_o_aff_w': _L1_cond_in['o_aff_w'], 'L1_cond_o_aff_b': _L1_cond_in['o_aff_b'], 'L1_cond_o_w': _L1_cond_in['o_w'], 'L1_cond_o_b': _L1_cond_in['o_b']}

def reference(x, cond_512, L0_cond_weight, L0_cond_bias, L0_cond_affine_w, L0_cond_affine_b, L1_cond_k_aff_w, L1_cond_k_aff_b, L1_cond_k_w, L1_cond_k_b, L1_cond_o_aff_w, L1_cond_o_aff_b, L1_cond_o_w, L1_cond_o_b):
    import jax
    import jax.numpy as jnp

    def _L0_cond_ref(x, w, weight, bias, affine_w, affine_b):
        import jax, jax.numpy as jnp
        import numpy as np
        W_DIM = 256
        CLAMP = 256.0
        B, L, C = x.shape
        gain = 1.0 / np.sqrt(W_DIM).astype(np.float32)
        styles = w @ (affine_w * gain).T + affine_b
        ws = weight[None, :, :] * styles[:, None, :]
        dcoefs = jax.lax.rsqrt(jnp.sum(ws * ws, axis=2) + 1e-08)
        xm = x * styles[:, None, :]
        y = jnp.einsum('blc,oc->blo', xm, weight)
        y = y * dcoefs[:, None, :]
        y = jnp.clip(y + bias, -CLAMP, CLAMP)
        return y

    def _L1_cond_ref(x, s, k_aff_w, k_aff_b, k_w, k_b, o_aff_w, o_aff_b, o_w, o_b):
        import jax, jax.numpy as jnp
        import numpy as np
        import math
        HEAD_NUM = 16
        EPS = 1e-08

        def modulated_linear(x, s, aff_w, aff_b, w, b):
            style = s @ aff_w.T + aff_b
            w_mod = w[None, :, :] * style[:, None, :]
            demod = jax.lax.rsqrt(jnp.sum(w_mod * w_mod, axis=2) + EPS)
            w_mod = w_mod * demod[:, :, None]
            return jnp.einsum('bni,boi->bno', x, w_mod) + b
        B, N, F = x.shape
        H = HEAD_NUM
        D = F // H
        kx = modulated_linear(x, s, k_aff_w, k_aff_b, k_w, k_b)
        kx = kx.reshape(B, N, H, D)
        q = k = v = kx
        scores = jnp.einsum('bnhd,bnjd->bnhj', q, k) / math.sqrt(D)
        A = jax.nn.softmax(scores, axis=-1)
        out = jnp.einsum('bnhj,bnjd->bnhd', A, v).reshape(B, N, F)
        out = modulated_linear(out, s, o_aff_w, o_aff_b, o_w, o_b)
        return out
    x = x + _L0_cond_ref(x, cond_512, L0_cond_weight, L0_cond_bias, L0_cond_affine_w, L0_cond_affine_b)
    x = x + _L1_cond_ref(x, cond_512, L1_cond_k_aff_w, L1_cond_k_aff_b, L1_cond_k_w, L1_cond_k_b, L1_cond_o_aff_w, L1_cond_o_aff_b, L1_cond_o_w, L1_cond_o_b)
    return x

_drawn_inputs = setup_inputs


def setup_inputs(seed=0):
    import zlib

    import numpy as np

    out = dict(_drawn_inputs(seed))
    spreads = {'L0_cond_affine_b': (1.0, 0.2),
     'L1_cond_k_aff_b': (1.0, 0.2),
     'L1_cond_k_b': (0.0, 0.1),
     'L1_cond_o_aff_b': (1.0, 0.2),
     'L1_cond_o_b': (0.0, 0.1)}
    factors = {}
    for name, (base, spread) in spreads.items():
        noise = np.random.default_rng([zlib.crc32(name.encode()), seed]).standard_normal(out[name].shape)
        drawn = base * np.exp(spread * noise) if base else spread * noise
        out[name] = jnp.asarray(drawn.astype(out[name].dtype))
    for name, factor in factors.items():
        out[name] = (out[name] * factor).astype(out[name].dtype)
    return out
```

```python
from contextlib import ExitStack

import concourse.bass as bass
from concourse import mybir

F32 = mybir.dt.float32
F32R = mybir.dt.float32r
ALU = mybir.AluOpType
ACT = mybir.ActivationFunctionType
AX_X = mybir.AxisListType.X

P = 128
HEADS = 16
EPS = 1e-8
CLAMP = 256.0
DMA = 16


def build(nc, xT, condT, wT, affT, aff_b, lin_b, block_ones, token_mask, head_diag, dim_eye, outT):
    F, NT = xT.shape
    SD, B = condT.shape
    HD = F // HEADS
    KB = F // P
    SB = SD // P
    HR = P // HD
    T = 256
    N = NT // T
    PER_BATCH = NT // B // T
    TB = T // HR
    TG = P // HEADS
    NG = T // TG
    GJ = NG // HR
    NC = HEADS + HD
    SU = NG // GJ
    PB = 512 // P
    NPB = GJ // PB
    W = TB // HR
    NLB = 3
    GAIN = (float(SD) ** -0.5, 1.0, 1.0)
    SCALE = float(HD) ** -0.5
    L0, K, O = range(3)
    assert HR == 4 and TG == 8 and GJ * NC <= 512 and NG * HEADS == 512 and W == 2 * GJ

    xT_v = xT.rearrange("(k p) t -> p k t", p=P)
    outT_v = outT.rearrange("(k p) t -> p k t", p=P)

    with ExitStack() as ctx:
        def sb(name, shape, dt=F32):
            return ctx.enter_context(nc.sbuf_tensor(name, [P] + shape, dt))

        def ps(name, shape):
            return ctx.enter_context(nc.psum_tensor(name, [P] + shape, F32))

        def sem(name):
            return ctx.enter_context(nc.semaphore(name))

        w_hi = [sb(f"w_hi{l}", [KB, F], F32R) for l in range(3)]
        w_lo = [sb(f"w_lo{l}", [KB, F], F32R) for l in range(3)]
        style = [sb(f"style{l}", [KB, B]) for l in range(3)]
        style_sq = [sb(f"style_sq{l}", [KB, B]) for l in range(3)]
        demod = [sb(f"demod{l}", [KB, B]) for l in range(3)]
        norm = [sb(f"norm{l}", [KB, B]) for l in range(3)]
        affb_sb = [sb(f"affb{l}", [KB]) for l in range(3)]
        bias_sb = [sb(f"bias{l}", [KB]) for l in range(3)]
        cond_sb = sb("cond", [SB, B])
        ones_f = sb("ones_f", [P])
        ones_r = sb("ones_r", [P], F32R)
        tok_mask = sb("tok_mask", [TG])
        diag = sb("diag", [HEADS])
        eye = sb("eye", [HD])
        x_sb = sb("x", [2, KB, T])
        x1_sb = sb("x1", [3, KB, T])
        x_hi, x_lo = sb("x_hi", [KB, T], F32R), sb("x_lo", [KB, T], F32R)
        x1_hi, x1_lo = sb("x1_hi", [KB, T], F32R), sb("x1_lo", [KB, T], F32R)
        kx_sb = sb("kx", [KB, T])
        k_rhs = sb("k_rhs", [NC, TB])
        k_bd = sb("k_bd", [HR * HEADS, TB])
        sv_sb = sb("sv", [NG, NC])
        mx = sb("mx", [NG])
        mx_hi, mx_lo = sb("mx_hi", [NG], F32R), sb("mx_lo", [NG], F32R)
        md_hi, md_lo = sb("md_hi", [NG, HEADS], F32R), sb("md_lo", [NG, HEADS], F32R)
        ex = sb("ex", [NG, HEADS])
        ex_hi, ex_lo = sb("ex_hi", [NG, HEADS], F32R), sb("ex_lo", [NG, HEADS], F32R)
        prob = sb("prob", [NG, HEADS])
        p_bd = sb("p_bd", [NG, TG, HEADS])
        y_sb = sb("y", [HEADS, HR, W])
        yr_sb = sb("yr", [KB, T])
        y_hi, y_lo = sb("y_hi", [KB, T], F32R), sb("y_lo", [KB, T], F32R)
        o_sb = sb("o", [2, KB, T])
        aff_v = [k_rhs[:, :, :].rearrange("p a b -> p (a b)")[:, l * SB * F:(l + 1) * SB * F]
                 .rearrange("p (s f) -> p s f", s=SB) for l in range(3)]
        pbd_flat = p_bd[:, :, :, :].rearrange("p a b c -> p (a b c)")
        w_raw = [pbd_flat[:, 0:KB * F], pbd_flat[:, KB * F:2 * KB * F], sb("w_raw2", [KB * F])[:, :]]
        w_raw = [w.rearrange("p (k f) -> p k f", k=KB) for w in w_raw]
        w_sq = sb("w_sq", [KB, F])

        lin_ps = ps("lin_ps", [NLB, 512])
        s_ps = ps("s_ps", [2, 512])
        cd_ps = ps("cd_ps", [512])
        y_ps = ps("y_ps", [NPB, 512])

        ld_const = [sem(f"ld_const{l}") for l in range(3)]
        ld_small = sem("ld_small")
        ld_x = [sem(f"ld_x{i}") for i in range(2)]
        rl_k = sem("rl_k")
        rl_bd = sem("rl_bd")
        rl_y = sem("rl_y")
        st_o = [sem(f"st_o{i}") for i in range(2)]
        g_zero = sem("g_zero")
        v_eye = sem("v_eye")
        pe_style, v_style = sem("pe_style"), sem("v_style")
        v_ssq, v_wsq = sem("v_ssq"), sem("v_wsq")
        pe_norm, v_norm, a_norm, v_demod = sem("pe_norm"), sem("v_norm"), sem("a_norm"), sem("v_demod")
        a_whi, v_wlo, a_ones = sem("a_whi"), sem("v_wlo"), sem("a_ones")
        pe_lin, a_lin = sem("pe_lin"), sem("a_lin")
        a_xhi, v_xlo = sem("a_xhi"), sem("v_xlo")
        v_clip, v_x1 = sem("v_clip"), sem("v_x1")
        a_x1hi, v_x1lo = sem("a_x1hi"), sem("v_x1lo")
        pe_s, a_sv = sem("pe_s"), sem("a_sv")
        v_max, v_mhi, v_mlo, v_diag = sem("v_max"), sem("v_mhi"), sem("v_mlo"), sem("v_diag")
        pe_c, v_sub, a_exp = sem("pe_c"), sem("v_sub"), sem("a_exp")
        v_ehi, v_elo, pe_d = sem("v_ehi"), sem("v_elo"), sem("pe_d")
        v_rec, v_prob, v_pbd = sem("v_rec"), sem("v_prob"), sem("v_pbd")
        pe_pv, a_y = sem("pe_pv"), sem("a_y")
        a_yhi, v_ylo = sem("a_yhi"), sem("v_ylo")
        v_out = sem("v_out")

        def pe_steps(i):
            steps = []
            if i < N:
                steps += [("lin", L0, i, m) for m in range(KB)]
            if i == 0:
                steps += [("setup", K)]
            if 0 <= i - 2 < N:
                steps += [("pv", i - 2)]
            if 0 <= i - 1 < N:
                steps += [("scores", i - 1)]
            k_blocks = [("lin", K, i, m) for m in range(KB)] if i < N else []
            o_blocks = [("lin", O, i - 2, m) for m in range(KB)] if 0 <= i - 2 < N else []
            if 0 <= i - 1 < N:
                k_blocks.insert(len(k_blocks) // 2, ("max", i - 1))
                o_blocks.insert(len(o_blocks) // 2, ("sum", i - 1))
            steps += k_blocks + o_blocks
            if i == 0:
                steps += [("setup", O)]
            return steps

        block_no = {}
        for i in range(N + 2):
            for step in pe_steps(i):
                if step[0] == "lin":
                    block_no[step[1:]] = len(block_no)

        def done(l, c, m):
            return block_no[(l, c, m)] + 1

        block = ctx.enter_context(nc.Block())

        @block.sync
        def _(sp):
            def load_x(c):
                if c >= 2:
                    sp.wait_ge(v_x1, 2 * (c - 1))
                sp.dma_start(x_sb[:, c % 2], xT_v[:, :, c * T:(c + 1) * T]).then_inc(ld_x[c % 2], DMA)

            sp.dma_start(cond_sb[:], condT.rearrange("(s p) b -> p s b", p=P)).then_inc(ld_small, DMA)
            sp.dma_start(aff_v[0], affT[0].rearrange("(s p) f -> p s f", p=P)).then_inc(ld_small, DMA)
            for src, dst in [(block_ones, ones_f), (token_mask, tok_mask), (head_diag, diag), (dim_eye, eye)]:
                sp.dma_start(dst[:], src).then_inc(ld_small, DMA)
            for l in range(3):
                sp.dma_start(affb_sb[l][:], aff_b[l]).then_inc(ld_small, DMA)
                sp.dma_start(bias_sb[l][:], lin_b[l]).then_inc(ld_small, DMA)
            for l in (1, 2):
                sp.dma_start(aff_v[l], affT[l].rearrange("(s p) f -> p s f", p=P)).then_inc(ld_small, DMA)
            load_x(0)
            for l in (1, 2):
                sp.dma_start(w_raw[l], wT[l].rearrange("(k p) f -> p k f", p=P)).then_inc(ld_const[l], DMA)

            for i in range(N + 2):
                if i + 1 < N:
                    load_x(i + 1)
                c = i - 2
                if 0 <= c < N:
                    sp.wait_ge(a_y, NPB * (c + 1))
                    if c:
                        sp.wait_ge(a_yhi, c)
                        sp.wait_ge(v_ylo, c)
                    y_v = y_sb[:, :, :, :].rearrange("p h b w -> p h (b w)")
                    for j in range(HR):
                        for hr in range(HR):
                            sp.dma_start(yr_sb[HD * hr:HD * (hr + 1), :, j * TB:(j + 1) * TB],
                                         y_v[HD * j:HD * (j + 1), hr::HR, :]).then_inc(rl_y, DMA)
                c = i
                if c < N:
                    sp.wait_ge(a_lin, done(K, c, KB - 1))
                    if c == 0:
                        sp.wait_ge(v_style, 3)
                        sp.wait_ge(g_zero, 1)
                    else:
                        sp.wait_ge(pe_s, SU * c)
                    for tb in range(HR):
                        for hr in range(HR):
                            sp.dma_start(k_rhs[HD * tb:HD * (tb + 1), hr:HEADS:HR, :],
                                         kx_sb[HD * hr:HD * (hr + 1), :, tb * TB:(tb + 1) * TB]).then_inc(rl_k, DMA)
                    sp.wait_ge(rl_k, DMA * HR * HR * (c + 1))
                    for tb in range(HR):
                        sp.dma_start(k_bd[HD * tb:HD * (tb + 1), tb * HEADS:(tb + 1) * HEADS, :],
                                     k_rhs[HD * tb:HD * (tb + 1), 0:HEADS, :]).then_inc(rl_bd, DMA)
                c = i - 2
                if 0 <= c < N:
                    sp.wait_ge(v_out, 2 * (c + 1))
                    sp.dma_start(outT_v[:, :, c * T:(c + 1) * T], o_sb[:, c % 2]).then_inc(st_o[c % 2], DMA)
            for b in range(2):
                sp.wait_ge(st_o[b], DMA * len(range(b, N, 2)))

        @block.gpsimd
        def _(pool):
            pool.memset(k_bd[:, :, :], 0.0).then_inc(g_zero, 1)

        @block.tensor
        def _(pe):
            operands = {L0: (x_hi, x_lo), K: (x1_hi, x1_lo), O: (y_hi, y_lo)}
            split = {L0: (a_xhi, v_xlo), K: (a_x1hi, v_x1lo), O: (a_yhi, v_ylo)}

            def linear(l, c, m):
                n = block_no[(l, c, m)]
                if m == 0:
                    pe.wait_ge(split[l][0], (c + 1) * (2 if l == K else 1))
                    pe.wait_ge(split[l][1], (c + 1) * (2 if l == K else 1))
                    if c == 0:
                        pe.wait_ge(a_whi, l + 1)
                        pe.wait_ge(v_wlo, l + 1)
                if n >= NLB:
                    pe.wait_ge(a_lin, n - NLB + 1)
                hi, lo = operands[l]
                passes = [(k, w, r) for k in range(KB)
                          for w, r in ((w_hi[l], hi), (w_hi[l], lo), (w_lo[l], hi))]
                for q, (k, w, r) in enumerate(passes):
                    mm = pe.matmul(lin_ps[:, n % NLB, 0:T], w[:, k, m * P:(m + 1) * P], r[:, k, :],
                                   start=(q == 0), stop=(q == len(passes) - 1))
                mm.then_inc(pe_lin, 1)

            def styles():
                pe.wait_ge(ld_small, DMA * SMALL)
                for l in range(3):
                    for m in range(KB):
                        for s in range(SB):
                            mm = pe.matmul(y_ps[:, 0, (l * KB + m) * B:(l * KB + m + 1) * B],
                                           aff_v[l][:, s, m * P:(m + 1) * P], cond_sb[:, s, :],
                                           start=(s == 0), stop=(s == SB - 1))
                    mm.then_inc(pe_style, 1)

            def norms(l):
                pe.wait_ge(v_ssq, l + 1)
                pe.wait_ge(v_wsq, l + 1)
                if l:
                    pe.wait_ge(v_norm, l)
                for m in range(KB):
                    for k in range(KB):
                        mm = pe.matmul(y_ps[:, 1, (l * KB + m) * B:(l * KB + m + 1) * B],
                                       w_sq[:, k, m * P:(m + 1) * P], style_sq[l][:, k, :],
                                       start=(k == 0), stop=(k == KB - 1))
                mm.then_inc(pe_norm, 1)

            def scores(c):
                pe.wait_ge(rl_bd, DMA * HR * (c + 1))
                if c == 0:
                    pe.wait_ge(v_eye, 1)
                for j in range(SU):
                    if SU * c + j >= 2:
                        pe.wait_ge(a_sv, SU * c + j - 1)
                    for q in range(GJ):
                        for u in range(2):
                            g = j * W + 2 * q + u
                            mm = pe.matmul(s_ps[64 * u:64 * u + 64, j % 2, q * NC:(q + 1) * NC],
                                           k_bd[:, :, g], k_rhs[:, :, g], start=True, stop=True)
                    mm.then_inc(pe_s, 1)

            def over_token(c, ready, hi, lo, raised):
                pe.wait_ge(ready, c + 1)
                for r in (hi, lo):
                    mm = pe.matmul(cd_ps[:, :], ones_r[:, :], r[:, :, :].rearrange("p g h -> p (g h)"),
                                   start=(r is hi), stop=(r is lo))
                mm.then_inc(raised, 1)

            def pv(c):
                pe.wait_ge(v_pbd, c + 1)
                if c == 0:
                    pe.wait_ge(v_norm, 3)
                for q in range(GJ):
                    if q % PB == 0 and c:
                        pe.wait_ge(a_y, NPB * (c - 1) + q // PB + 1)
                    for j in range(HR):
                        grp = j * GJ + q
                        mm = pe.matmul(y_ps[HD * j:HD * (j + 1), q // PB, (q % PB) * P:(q % PB + 1) * P],
                                       sv_sb[:, grp, HEADS:NC],
                                       p_bd[:, grp].rearrange("p t h -> p (t h)"), start=True, stop=True)
                    if q % PB == PB - 1:
                        mm.then_inc(pe_pv, 1)

            styles()
            norms(L0)
            for i in range(N + 2):
                for step in pe_steps(i):
                    if step[0] == "lin":
                        linear(*step[1:])
                    elif step[0] == "setup":
                        norms(step[1])
                    elif step[0] == "pv":
                        pv(step[1])
                    elif step[0] == "scores":
                        scores(step[1])
                    elif step[0] == "max":
                        if step[1] == 0:
                            pe.wait_ge(a_ones, 1)
                        else:
                            pe.wait_ge(v_rec, step[1])
                        over_token(step[1], v_diag, md_hi, md_lo, pe_c)
                    else:
                        over_token(step[1], v_elo, ex_hi, ex_lo, pe_d)

        @block.scalar
        def _(act):
            def evacuate(l, c, m, out):
                act.wait_ge(pe_lin, done(l, c, m))
                b = c // PER_BATCH
                src = lin_ps[:, block_no[(l, c, m)] % NLB, 0:T]
                if l == O:
                    src = src.rearrange("p (j b w) -> p j b w", j=HR, b=HR)
                act.activation(out, src, ACT.Identity, bias=bias_sb[l][:, m:m + 1],
                               scale=demod[l][:, m, b:b + 1]).then_inc(a_lin, 1)

            def hi_part(l, c, out, src, k0, k1, raised):
                b = c // PER_BATCH
                for k in range(k0, k1):
                    a = act.activation(out[:, k], src[:, k], ACT.Copy, scale=style[l][:, k, b:b + 1])
                a.then_inc(raised, 1)

            def x_hi_of(c):
                act.wait_ge(ld_x[c % 2], DMA * (c // 2 + 1))
                if c:
                    act.wait_ge(pe_lin, done(L0, c - 1, KB - 1))
                hi_part(L0, c, x_hi, x_sb[:, c % 2], 0, KB, a_xhi)

            def layer_setup(l):
                act.wait_ge(ld_const[l], DMA)
                act.activation(w_hi[l][:], w_raw[l], ACT.Copy).then_inc(a_whi, 1)

            def roots(l):
                act.wait_ge(v_norm, l + 1)
                act.activation(norm[l][:], norm[l][:], ACT.Sqrt).then_inc(a_norm, 1)

            act.dma_start(w_raw[0], wT[0].rearrange("(k p) f -> p k f", p=P)).then_inc(ld_const[0], DMA)
            layer_setup(L0)
            act.wait_ge(v_style, 1)
            x_hi_of(0)
            layer_setup(K)
            layer_setup(O)
            act.wait_ge(ld_small, DMA * SMALL)
            act.activation(ones_r[:], ones_f[:], ACT.Copy).then_inc(a_ones, 1)
            roots(L0)
            act.wait_ge(v_demod, 1)

            for i in range(N + 2):
                if i < N:
                    if i >= 3:
                        act.wait_ge(v_out, 2 * (i - 2))
                    for m in range(KB):
                        evacuate(L0, i, m, x1_sb[:, i % 3, m])
                c = i - 2
                if 0 <= c < N:
                    if c:
                        act.wait_ge(rl_y, DMA * HR * HR * c)
                    for k in range(NPB):
                        act.wait_ge(pe_pv, NPB * c + k + 1)
                        act.activation(y_sb[:, :, :, k * 2 * PB:(k + 1) * 2 * PB].rearrange("p h b w -> p w b h"),
                                       y_ps[:, k, :].rearrange("p (w b h) -> p w b h", b=HR, h=HEADS),
                                       ACT.Copy).then_inc(a_y, 1)
                if i < N:
                    if i == 0:
                        roots(K)
                        act.wait_ge(v_demod, 2)
                    else:
                        act.wait_ge(pe_lin, done(K, i - 1, KB - 1))
                    for h in range(2):
                        act.wait_ge(v_x1, 2 * i + h + 1)
                        hi_part(K, i, x1_hi, x1_sb[:, i % 3], h * KB // 2, (h + 1) * KB // 2, a_x1hi)
                for j in range(SU):
                    c = i - 1
                    if 0 <= c < N:
                        if j == 0 and c:
                            act.wait_ge(pe_pv, NPB * c)
                        act.wait_ge(pe_s, SU * c + j + 1)
                        act.activation(sv_sb[:, j * GJ:(j + 1) * GJ, :],
                                       s_ps[:, j % 2, 0:GJ * NC].rearrange("p (g n) -> p g n", n=NC),
                                       ACT.Copy).then_inc(a_sv, 1)
                    c = i - 2
                    if 0 <= c < N and j == 1:
                        act.wait_ge(rl_y, DMA * HR * HR * (c + 1))
                        if c:
                            act.wait_ge(pe_lin, done(O, c - 1, KB - 1))
                        hi_part(O, c, y_hi, yr_sb, 0, KB, a_yhi)
                if i + 1 < N:
                    x_hi_of(i + 1)
                for m in range(KB):
                    if i < N:
                        if m == 0 and i:
                            act.wait_ge(rl_k, DMA * HR * HR * i)
                        evacuate(K, i, m, kx_sb[:, m])
                    c = i - 1
                    if 0 <= c < N and m == KB - 2:
                        act.wait_ge(v_sub, c + 1)
                        act.activation(ex[:], ex[:], ACT.Exp, scale=SCALE).then_inc(a_exp, 1)
                if i == 0:
                    roots(O)
                    act.wait_ge(v_demod, 3)
                c = i - 2
                if 0 <= c < N:
                    if c >= 2:
                        act.wait_ge(st_o[c % 2], DMA * (c // 2))
                    for m in range(KB):
                        evacuate(O, c, m, o_sb[:, c % 2, m].rearrange("p (b j w) -> p j b w", b=HR, j=HR))

        @block.vector
        def _(dve):
            def lo_part(l, c, out, src, hi, k0, k1, raised):
                b = c // PER_BATCH
                for k in range(k0, k1):
                    v = dve.scalar_tensor_tensor(out=out[:, k], in0=src[:, k], scalar=style[l][:, k, b:b + 1],
                                                 in1=hi[:, k], op0=ALU.mult, op1=ALU.subtract)
                v.then_inc(raised, 1)

            def x_lo_of(c):
                dve.wait_ge(a_xhi, c + 1)
                lo_part(L0, c, x_lo, x_sb[:, c % 2], x_hi, 0, KB, v_xlo)

            def style_of(l):
                dve.wait_ge(pe_style, 3)
                dve.scalar_tensor_tensor(
                    out=style[l][:], in0=y_ps[:, 0, l * KB * B:(l + 1) * KB * B].rearrange("p (k b) -> p k b", b=B),
                    scalar=GAIN[l], in1=affb_sb[l][:].unsqueeze(2).to_broadcast([P, KB, B]),
                    op0=ALU.mult, op1=ALU.add).then_inc(v_style, 1)
                dve.wait_ge(v_style, l + 1)
                dve.tensor_tensor(style_sq[l][:], style[l][:], style[l][:], ALU.mult).then_inc(v_ssq, 1)

            def squares(l):
                dve.wait_ge(ld_const[l], DMA)
                if l:
                    dve.wait_ge(pe_norm, l)
                dve.tensor_tensor(w_sq[:], w_raw[l], w_raw[l], ALU.mult).then_inc(v_wsq, 1)

            def weights_lo(l):
                dve.wait_ge(a_whi, l + 1)
                dve.tensor_tensor(w_lo[l][:], w_raw[l], w_hi[l][:], ALU.subtract).then_inc(v_wlo, 1)

            def demod_of(l):
                dve.wait_ge(pe_norm, l + 1)
                dve.tensor_scalar(norm[l][:], y_ps[:, 1, l * KB * B:(l + 1) * KB * B]
                                  .rearrange("p (k b) -> p k b", b=B), EPS, None, ALU.add).then_inc(v_norm, 1)
                dve.wait_ge(a_norm, l + 1)
                dve.reciprocal(demod[l][:], norm[l][:]).then_inc(v_demod, 1)

            dve.wait_ge(ld_small, DMA * SMALL)
            for l in range(3):
                style_of(l)
            squares(L0)
            weights_lo(L0)
            x_lo_of(0)
            demod_of(L0)
            squares(K)
            weights_lo(K)
            dve.wait_ge(v_style, 3)
            dve.tensor_copy(k_rhs[:, HEADS:NC, :], eye[:].unsqueeze(2).to_broadcast([P, HD, TB])).then_inc(v_eye, 1)

            for i in range(N + 2):
                half = KB // 2
                if i < N:
                    for h in range(2):
                        x1h = x1_sb[:, i % 3, h * half:(h + 1) * half]
                        dve.wait_ge(a_lin, done(L0, i, (h + 1) * half - 1))
                        dve.tensor_scalar(x1h, x1h, CLAMP, -CLAMP, ALU.min, ALU.max).then_inc(v_clip, 1)
                        dve.wait_ge(v_clip, 2 * i + h + 1)
                        dve.tensor_tensor(x1h, x1h, x_sb[:, i % 2, h * half:(h + 1) * half],
                                          ALU.add).then_inc(v_x1, 1)
                    if i == 0:
                        demod_of(K)
                        squares(O)
                        weights_lo(O)
                    for h in range(2):
                        dve.wait_ge(a_x1hi, 2 * i + h + 1)
                        lo_part(K, i, x1_lo, x1_sb[:, i % 3], x1_hi, h * half, (h + 1) * half, v_x1lo)
                c = i - 2
                if 0 <= c < N:
                    dve.wait_ge(a_yhi, c + 1)
                    lo_part(O, c, y_lo, yr_sb, y_hi, 0, KB, v_ylo)
                c = i - 1
                if 0 <= c < N:
                    dve.wait_ge(a_sv, SU * (c + 1))
                    dve.tensor_reduce(out=mx[:], in_=sv_sb[:, :, 0:HEADS], axis=AX_X, op=ALU.max).then_inc(v_max, 1)
                    dve.wait_ge(v_max, c + 1)
                    dve.tensor_copy(mx_hi[:], mx[:]).then_inc(v_mhi, 1)
                    dve.wait_ge(v_mhi, c + 1)
                    dve.tensor_tensor(mx_lo[:], mx[:], mx_hi[:], ALU.subtract).then_inc(v_mlo, 1)
                    dve.wait_ge(v_mlo, c + 1)
                    for src, dst in ((mx_hi, md_hi), (mx_lo, md_lo)):
                        v = dve.tensor_tensor(dst[:], src[:].unsqueeze(2).to_broadcast([P, NG, HEADS]),
                                              diag[:].unsqueeze(1).to_broadcast([P, NG, HEADS]), ALU.mult)
                    v.then_inc(v_diag, 1)
                if i + 1 < N:
                    x_lo_of(i + 1)
                if 0 <= c < N:
                    dve.wait_ge(pe_c, c + 1)
                    dve.tensor_tensor(ex[:], sv_sb[:, :, 0:HEADS],
                                      cd_ps[:, :].rearrange("p (g h) -> p g h", h=HEADS),
                                      ALU.subtract).then_inc(v_sub, 1)
                    dve.wait_ge(a_exp, c + 1)
                    dve.tensor_copy(ex_hi[:], ex[:]).then_inc(v_ehi, 1)
                    dve.wait_ge(v_ehi, c + 1)
                    dve.tensor_tensor(ex_lo[:], ex[:], ex_hi[:], ALU.subtract).then_inc(v_elo, 1)
                c2 = i - 2

                def finish(h):
                    oh = o_sb[:, c2 % 2, h * half:(h + 1) * half]
                    dve.wait_ge(a_lin, done(O, c2, (h + 1) * half - 1))
                    dve.tensor_tensor(oh, oh, x1_sb[:, c2 % 3, h * half:(h + 1) * half], ALU.add).then_inc(v_out, 1)

                if i == 0:
                    demod_of(O)
                if 0 <= c < N:
                    dve.wait_ge(pe_d, c + 1)
                    dve.reciprocal(prob[:], cd_ps[:, :].rearrange("p (g h) -> p g h", h=HEADS)).then_inc(v_rec, 1)
                if 0 <= c2 < N:
                    finish(0)
                if 0 <= c < N:
                    dve.wait_ge(v_rec, c + 1)
                    dve.tensor_tensor(prob[:], prob[:], ex[:], ALU.mult).then_inc(v_prob, 1)
                    dve.wait_ge(v_prob, c + 1)
                    for t in range(TG):
                        v = dve.tensor_scalar(p_bd[:, :, t, :], prob[:], tok_mask[:, t:t + 1], None, ALU.mult)
                    v.then_inc(v_pbd, 1)
                if 0 <= c2 < N:
                    finish(1)


SMALL = 14

_LAYERS = (("L0_cond_weight", "L0_cond_affine_w", "L0_cond_affine_b", "L0_cond_bias"),
           ("L1_cond_k_w", "L1_cond_k_aff_w", "L1_cond_k_aff_b", "L1_cond_k_b"),
           ("L1_cond_o_w", "L1_cond_o_aff_w", "L1_cond_o_aff_b", "L1_cond_o_b"))


def kernel(**inputs):
    import numpy as np
    import concourse.bacc as bacc
    from concourse.bass_utils import run_bass_kernel_spmd

    x = np.asarray(inputs["x"])
    B, L, F = x.shape
    part = np.arange(P)
    cols = lambda v: np.ascontiguousarray(np.asarray(v).reshape(F // P, P).T)
    turned = lambda a: np.ascontiguousarray(np.asarray(a).T)
    arrays = {"xT": turned(x.reshape(B * L, F)), "condT": turned(inputs["cond_512"])}
    for l, (w, aw, ab, b) in enumerate(_LAYERS):
        arrays[f"wT{l}"], arrays[f"affT{l}"] = turned(inputs[w]), turned(inputs[aw])
        arrays[f"aff_b{l}"], arrays[f"lin_b{l}"] = cols(inputs[ab]), cols(inputs[b])
    HD = F // HEADS
    arrays["block_ones"] = (part[:, None] // HEADS == part[None, :] // HEADS).astype(np.float32)
    arrays["token_mask"] = (part[:, None] // HEADS == np.arange(P // HEADS)[None, :]).astype(np.float32)
    arrays["head_diag"] = (part[:, None] % HEADS == np.arange(HEADS)[None, :]).astype(np.float32)
    arrays["dim_eye"] = (part[:, None] % HD == np.arange(HD)[None, :]).astype(np.float32)

    nc = bacc.Bacc("TRN2", target_bir_lowering=False, num_devices=1)
    d = {n: nc.dram_tensor(n, a.shape, mybir.dt.from_np(a.dtype), kind="ExternalInput").ap() for n, a in arrays.items()}
    outT = nc.dram_tensor("outT", (F, B * L), F32, kind="ExternalOutput").ap()
    three = lambda n: [d[f"{n}{l}"] for l in range(3)]
    build(nc, d["xT"], d["condT"], three("wT"), three("affT"), three("aff_b"), three("lin_b"),
          d["block_ones"], d["token_mask"], d["head_diag"], d["dim_eye"], outT)
    r = run_bass_kernel_spmd(nc, [arrays], core_ids=[0])
    return np.ascontiguousarray(r.results[0]["outT"].T).reshape(B, L, F)
```

```python
from contextlib import ExitStack

import concourse.bass as bass
from concourse import mybir

F32 = mybir.dt.float32
F32R = mybir.dt.float32r
ALU = mybir.AluOpType
ACT = mybir.ActivationFunctionType
AX_X = mybir.AxisListType.X

P = 128
HEADS = 16
EPS = 1e-8
CLAMP = 256.0
DMA = 16


def build(nc, xT, condT, wT, affT, aff_b, lin_b, block_ones, token_mask, head_diag, dim_eye, outT):
    F, NT = xT.shape
    SD, B = condT.shape
    HD = F // HEADS
    KB = F // P
    SB = SD // P
    HR = P // HD
    T = 256
    N = NT // T
    PER_BATCH = NT // B // T
    TB = T // HR
    TG = P // HEADS
    NG = T // TG
    GJ = NG // HR
    NC = HEADS + HD
    SU = NG // GJ
    PB = 512 // P
    NPB = GJ // PB
    W = TB // HR
    DEPTH = 4
    NX1 = DEPTH + 1
    NLB = 3
    GAIN = (float(SD) ** -0.5, 1.0, 1.0)
    SCALE = float(HD) ** -0.5
    L0, K, O = range(3)
    assert HR == 4 and TG == 8 and GJ * NC <= 512 and NG * HEADS == 512 and W == 2 * GJ

    xT_v = xT.rearrange("(k p) t -> p k t", p=P)
    outT_v = outT.rearrange("(k p) t -> p k t", p=P)

    with ExitStack() as ctx:
        def sb(name, shape, dt=F32):
            return ctx.enter_context(nc.sbuf_tensor(name, [P] + shape, dt))

        def ps(name, shape):
            return ctx.enter_context(nc.psum_tensor(name, [P] + shape, F32))

        def sem(name):
            return ctx.enter_context(nc.semaphore(name))

        w_hi = [sb(f"w_hi{l}", [KB, F], F32R) for l in range(3)]
        w_lo = [sb(f"w_lo{l}", [KB, F], F32R) for l in range(3)]
        style = [sb(f"style{l}", [KB, B]) for l in range(3)]
        style_sq = [sb(f"style_sq{l}", [KB, B]) for l in range(3)]
        demod = [sb(f"demod{l}", [KB, B]) for l in range(3)]
        norm = [sb(f"norm{l}", [KB, B]) for l in range(3)]
        affb_sb = [sb(f"affb{l}", [KB]) for l in range(3)]
        bias_sb = [sb(f"bias{l}", [KB]) for l in range(3)]
        cond_sb = sb("cond", [SB, B])
        ones_f = sb("ones_f", [P])
        ones_r = sb("ones_r", [P], F32R)
        tok_mask = sb("tok_mask", [TG])
        diag = sb("diag", [HEADS])
        eye = sb("eye", [HD])
        x_sb = sb("x", [2, KB, T])
        x1_sb = sb("x1", [NX1, KB, T])
        x_hi, x_lo = sb("x_hi", [KB, T], F32R), sb("x_lo", [KB, T], F32R)
        x1_hi, x1_lo = sb("x1_hi", [KB, T], F32R), sb("x1_lo", [KB, T], F32R)
        kx_sb = sb("kx", [2, KB, T])
        k_rhs = sb("k_rhs", [NC, TB])
        k_bd = sb("k_bd", [HR * HEADS, TB])
        sv_sb = sb("sv", [2, NG, NC])
        mx = sb("mx", [NG])
        mx_hi, mx_lo = sb("mx_hi", [NG], F32R), sb("mx_lo", [NG], F32R)
        md_hi, md_lo = sb("md_hi", [NG, HEADS], F32R), sb("md_lo", [NG, HEADS], F32R)
        ex = sb("ex", [NG, HEADS])
        ex_hi, ex_lo = sb("ex_hi", [NG, HEADS], F32R), sb("ex_lo", [NG, HEADS], F32R)
        rcp = sb("rcp", [NG, HEADS])
        err = sb("err", [NG, HEADS])
        prob = sb("prob", [NG, HEADS])
        p_bd = sb("p_bd", [NG, TG, HEADS])
        y_sb = sb("y", [HEADS, HR, W])
        yr_sb = sb("yr", [KB, T])
        y_hi, y_lo = sb("y_hi", [2, KB, T], F32R), sb("y_lo", [2, KB, T], F32R)
        o_sb = sb("o", [2, KB, T])
        def halves(t, a, b, n=2):
            names = [f"d{d}" for d in range(len(t.shape) - 1)]
            flat = t.rearrange(f"p {' '.join(names)} -> p ({' '.join(names)})")
            return [flat[:, h * a * b:(h + 1) * a * b].rearrange("p (a b) -> p a b", a=a) for h in range(n)]

        aff_v = [halves(t, SB, F, 1)[0] for t in (o_sb[:, 0], y_sb[:, :, :, :], yr_sb[:, :, :])]
        w_raw = halves(p_bd[:, :, :, :], KB, F) + halves(sv_sb[:, :, :, :], KB, F, 1)
        w_sq = halves(k_bd[:, :, :], KB, F, 1) + halves(x1_sb[:, 1:NX1], KB, F)

        lin_ps = ps("lin_ps", [NLB, 512])
        s_ps = ps("s_ps", [2, 512])
        cd_ps = ps("cd_ps", [512])
        y_ps = ps("y_ps", [NPB, 512])

        ld_const = [sem(f"ld_const{l}") for l in range(3)]
        ld_first, ld_small = sem("ld_first"), sem("ld_small")
        ld_x = [sem(f"ld_x{i}") for i in range(2)]
        ld_kbd = sem("ld_kbd")
        st_o = [sem(f"st_o{i}") for i in range(2)]
        g_zero = sem("g_zero")
        v_eye = sem("v_eye")
        pe_style, v_style = sem("pe_style"), sem("v_style")
        v_ssq, v_wsq, g_wsq = sem("v_ssq"), sem("v_wsq"), sem("g_wsq")
        pe_norm, v_norm, a_norm, v_demod = sem("pe_norm"), sem("v_norm"), sem("a_norm"), sem("v_demod")
        a_whi, v_wlo, a_ones = sem("a_whi"), sem("v_wlo"), sem("a_ones")
        pe_lin, a_lin = sem("pe_lin"), sem("a_lin")
        a_xhi, v_xlo = sem("a_xhi"), sem("v_xlo")
        v_clip, v_x1 = sem("v_clip"), sem("v_x1")
        a_x1hi, v_x1lo = sem("a_x1hi"), sem("v_x1lo")
        a_krhs = sem("a_krhs")
        pe_s, a_sv = sem("pe_s"), sem("a_sv")
        v_max, v_mhi, v_mlo, v_diag = sem("v_max"), sem("v_mhi"), sem("v_mlo"), sem("v_diag")
        pe_c, v_sub, a_exp = sem("pe_c"), sem("v_sub"), sem("a_exp")
        v_ehi, v_elo, pe_d = sem("v_ehi"), sem("v_elo"), sem("pe_d")
        a_ln, a_rcp, v_err, v_rcp = sem("a_ln"), sem("a_rcp"), sem("v_err"), sem("v_rcp")
        v_prob, v_pbd = sem("v_prob"), sem("v_pbd")
        pe_pv, a_y, v_yr = sem("pe_pv"), sem("a_y"), sem("v_yr")
        a_yhi, v_ylo = sem("a_yhi"), sem("v_ylo")
        v_out = sem("v_out")

        def pe_steps(i):
            def blocks(l, c):
                return [("lin", l, c, m) for m in range(KB)] if 0 <= c < N else []

            def one(step, c):
                return [(step, c)] if 0 <= c < N else []

            l0, k, h = blocks(L0, i), blocks(K, i), KB // 2
            o = blocks(O, i - 4)
            return (l0[:h] + one("max", i - 2) + l0[h:] + [("setup", K)] * (i == 0) + [("setup", O)] * (i == 1)
                    + o[:1] + one("sum", i - 2) + o[1:] + k
                    + one("scores", i - 1) + one("pv", i - 2))

        block_no = {}
        ITER = N + DEPTH
        for i in range(ITER):
            for step in pe_steps(i):
                if step[0] == "lin":
                    block_no[step[1:]] = len(block_no)

        def done(l, c, m):
            return block_no[(l, c, m)] + 1

        block = ctx.enter_context(nc.Block())

        @block.sync
        def _(sp):
            def load_x(c):
                if c >= 2:
                    sp.wait_ge(v_x1, 2 * (c - 1))
                sp.dma_start(x_sb[:, c % 2], xT_v[:, :, c * T:(c + 1) * T]).then_inc(ld_x[c % 2], DMA)

            def load_affine(l, landed):
                sp.dma_start(aff_v[l], affT[l].rearrange("(s p) f -> p s f", p=P)).then_inc(landed, DMA)
                sp.dma_start(affb_sb[l][:], aff_b[l]).then_inc(landed, DMA)

            sp.dma_start(cond_sb[:], condT.rearrange("(s p) b -> p s b", p=P)).then_inc(ld_first, DMA)
            load_affine(L0, ld_first)
            load_x(0)
            for l in (K, O):
                sp.dma_start(w_raw[l], wT[l].rearrange("(k p) f -> p k f", p=P)).then_inc(ld_const[l], DMA)
                load_affine(l, ld_small)
            for l in range(3):
                sp.dma_start(bias_sb[l][:], lin_b[l]).then_inc(ld_small, DMA)
            for src, dst in [(block_ones, ones_f), (token_mask, tok_mask), (head_diag, diag), (dim_eye, eye)]:
                sp.dma_start(dst[:], src).then_inc(ld_small, DMA)

            for i in range(ITER):
                if i + 1 < N:
                    load_x(i + 1)
                c = i - 1
                if 0 <= c < N:
                    if c == 0:
                        sp.wait_ge(g_zero, 1)
                    else:
                        sp.wait_ge(pe_s, SU * c)
                    for tb in range(HR):
                        sp.wait_ge(a_krhs, 2 * (HR * c + tb + 1))
                        sp.dma_start(k_bd[HD * tb:HD * (tb + 1), tb * HEADS:(tb + 1) * HEADS, :],
                                     k_rhs[HD * tb:HD * (tb + 1), 0:HEADS, :]).then_inc(ld_kbd, DMA)
                c = i - 4
                if 0 <= c < N:
                    sp.wait_ge(v_out, 2 * (c + 1))
                    sp.dma_start(outT_v[:, :, c * T:(c + 1) * T], o_sb[:, c % 2]).then_inc(st_o[c % 2], DMA)
            for b in range(2):
                sp.wait_ge(st_o[b], DMA * len(range(b, N, 2)))

        @block.gpsimd
        def _(pool):
            for l in (K, O):
                pool.wait_ge(ld_const[l], DMA)
                pool.tensor_tensor(w_sq[l], w_raw[l], w_raw[l], ALU.mult).then_inc(g_wsq, 1)
            pool.wait_ge(pe_norm, 1)
            pool.memset(k_bd[:, :, :], 0.0).then_inc(g_zero, 1)

        @block.tensor
        def _(pe):
            operands = {L0: (x_hi, x_lo), K: (x1_hi, x1_lo)}
            split = {L0: (a_xhi, v_xlo), K: (a_x1hi, v_x1lo), O: (a_yhi, v_ylo)}

            def linear(l, c, m):
                n = block_no[(l, c, m)]
                if m == 0:
                    pe.wait_ge(split[l][0], 2 * (c + 1))
                    pe.wait_ge(split[l][1], 2 * (c + 1))
                    if c == 0:
                        pe.wait_ge(a_whi, l + 1)
                        pe.wait_ge(v_wlo, l + 1)
                if n >= NLB:
                    pe.wait_ge(a_lin, n - NLB + 1)
                hi, lo = (y_hi[:, c % 2], y_lo[:, c % 2]) if l == O else operands[l]
                passes = [(k, w, r) for k in range(KB)
                          for w, r in ((w_hi[l], hi), (w_hi[l], lo), (w_lo[l], hi))]
                for q, (k, w, r) in enumerate(passes):
                    mm = pe.matmul(lin_ps[:, n % NLB, 0:T], w[:, k, m * P:(m + 1) * P], r[:, k, :],
                                   start=(q == 0), stop=(q == len(passes) - 1))
                mm.then_inc(pe_lin, 1)

            def styles(l):
                pe.wait_ge(ld_first, DMA * FIRST)
                if l:
                    pe.wait_ge(ld_small, DMA * SMALL)
                    pe.wait_ge(v_style, l)
                for m in range(KB):
                    for s in range(SB):
                        mm = pe.matmul(y_ps[:, 0, (l * KB + m) * B:(l * KB + m + 1) * B],
                                       aff_v[l][:, s, m * P:(m + 1) * P], cond_sb[:, s, :],
                                       start=(s == 0), stop=(s == SB - 1))
                mm.then_inc(pe_style, 1)

            def norms(l):
                pe.wait_ge(v_ssq, l + 1)
                if l == L0:
                    pe.wait_ge(v_wsq, 1)
                else:
                    pe.wait_ge(g_wsq, l)
                    pe.wait_ge(v_norm, l)
                for m in range(KB):
                    for k in range(KB):
                        mm = pe.matmul(y_ps[:, 1, (l * KB + m) * B:(l * KB + m + 1) * B],
                                       w_sq[l][:, k, m * P:(m + 1) * P], style_sq[l][:, k, :],
                                       start=(k == 0), stop=(k == KB - 1))
                mm.then_inc(pe_norm, 1)

            def scores(c):
                pe.wait_ge(ld_kbd, DMA * HR * (c + 1))
                if c == 0:
                    pe.wait_ge(v_eye, 1)
                for j in range(SU):
                    if SU * c + j >= 2:
                        pe.wait_ge(a_sv, SU * c + j - 1)
                    for q in range(GJ):
                        for u in range(2):
                            g = j * W + 2 * q + u
                            mm = pe.matmul(s_ps[64 * u:64 * u + 64, j % 2, q * NC:(q + 1) * NC],
                                           k_bd[:, :, g], k_rhs[:, :, g], start=True, stop=True)
                    mm.then_inc(pe_s, 1)

            def over_token(c, ready, hi, lo, raised):
                pe.wait_ge(ready, c + 1)
                for r in (hi, lo):
                    mm = pe.matmul(cd_ps[:, :], ones_r[:, :], r[:, :, :].rearrange("p g h -> p (g h)"),
                                   start=(r is hi), stop=(r is lo))
                mm.then_inc(raised, 1)

            def pv(c):
                pe.wait_ge(v_pbd, c + 1)
                if c == 0:
                    pe.wait_ge(v_norm, 3)
                for q in range(GJ):
                    if q % PB == 0 and c:
                        pe.wait_ge(a_y, NPB * (c - 1) + q // PB + 1)
                    for j in range(HR):
                        grp = j * GJ + q
                        mm = pe.matmul(y_ps[HD * j:HD * (j + 1), q // PB, (q % PB) * P:(q % PB + 1) * P],
                                       sv_sb[:, c % 2, grp, HEADS:NC],
                                       p_bd[:, grp].rearrange("p t h -> p (t h)"), start=True, stop=True)
                    if q % PB == PB - 1:
                        mm.then_inc(pe_pv, 1)

            styles(L0)
            norms(L0)
            for i in range(ITER):
                for step in pe_steps(i):
                    if step[0] == "lin":
                        linear(*step[1:])
                    elif step[0] == "setup":
                        styles(step[1])
                        norms(step[1])
                    elif step[0] == "pv":
                        pv(step[1])
                    elif step[0] == "scores":
                        scores(step[1])
                    elif step[0] == "max":
                        if step[1] == 0:
                            pe.wait_ge(a_ones, 1)
                        else:
                            pe.wait_ge(v_err, step[1])
                        over_token(step[1], v_diag, md_hi, md_lo, pe_c)
                    else:
                        over_token(step[1], v_elo, ex_hi, ex_lo, pe_d)

        @block.scalar
        def _(act):
            def evacuate(l, c, m, out):
                act.wait_ge(pe_lin, done(l, c, m))
                b = c // PER_BATCH
                src = lin_ps[:, block_no[(l, c, m)] % NLB, 0:T]
                if l == O:
                    src = src.rearrange("p (j b w) -> p j b w", j=HR, b=HR)
                act.activation(out, src, ACT.Identity, bias=bias_sb[l][:, m:m + 1],
                               scale=demod[l][:, m, b:b + 1]).then_inc(a_lin, 1)

            def hi_part(l, c, h, out, src, raised):
                b = c // PER_BATCH
                for k in range(h * KB // 2, (h + 1) * KB // 2):
                    a = act.activation(out[:, k], src[:, k], ACT.Copy, scale=style[l][:, k, b:b + 1])
                a.then_inc(raised, 1)

            def x_hi_of(c, h):
                act.wait_ge(ld_x[c % 2], DMA * (c // 2 + 1))
                if c:
                    act.wait_ge(pe_lin, done(L0, c - 1, KB - 1))
                hi_part(L0, c, h, x_hi, x_sb[:, c % 2], a_xhi)

            def layer_setup(l):
                act.wait_ge(ld_const[l], DMA)
                act.activation(w_hi[l][:], w_raw[l], ACT.Copy).then_inc(a_whi, 1)

            def roots(l):
                act.wait_ge(v_norm, l + 1)
                act.activation(norm[l][:], norm[l][:], ACT.Sqrt).then_inc(a_norm, 1)

            def copy_k(c, part):
                tb, h = part // 2, part % 2
                if part == 0:
                    act.wait_ge(a_lin, done(K, c, KB - 1))
                    if c:
                        act.wait_ge(pe_s, SU * c)
                for hr in range(h * HR // 2, (h + 1) * HR // 2):
                    a = act.activation(k_rhs[HD * tb:HD * (tb + 1), hr:HEADS:HR, :],
                                       kx_sb[HD * hr:HD * (hr + 1), c % 2, :, tb * TB:(tb + 1) * TB], ACT.Copy)
                a.then_inc(a_krhs, 1)

            act.dma_start(w_raw[0], wT[0].rearrange("(k p) f -> p k f", p=P)).then_inc(ld_const[0], DMA)
            layer_setup(L0)
            act.wait_ge(v_style, 1)
            x_hi_of(0, 0)
            x_hi_of(0, 1)
            roots(L0)
            layer_setup(K)
            act.wait_ge(ld_small, DMA * SMALL)
            act.activation(ones_r[:], ones_f[:], ACT.Copy).then_inc(a_ones, 1)
            act.wait_ge(v_demod, 1)

            def roots_of_k(_):
                roots(K)
                act.wait_ge(v_demod, 2)

            def roots_of_o(_):
                layer_setup(O)
                roots(O)
                act.preload_act_table_set("natural_log_exp_and_others")
                act.wait_ge(v_demod, 3)

            def guess_reciprocal(c):
                act.wait_ge(pe_d, c + 1)
                act.activation(rcp[:], cd_ps[:, :].rearrange("p (g h) -> p g h", h=HEADS), ACT.Ln).then_inc(a_ln, 1)
                act.wait_ge(a_ln, c + 1)
                act.activation(rcp[:], rcp[:], ACT.Exp, scale=-1.0).then_inc(a_rcp, 1)

            def x1_hi_of(c, h):
                if c and h == 0:
                    act.wait_ge(pe_lin, done(K, c - 1, KB - 1))
                act.wait_ge(v_x1, 2 * c + h + 1)
                hi_part(K, c, h, x1_hi, x1_sb[:, c % NX1], a_x1hi)

            def y_hi_of(c, h):
                act.wait_ge(v_yr, c + 1)
                if c >= 2:
                    act.wait_ge(pe_lin, done(O, c - 2, KB - 1))
                hi_part(O, c, h, y_hi[:, c % 2], yr_sb, a_yhi)

            def evacuate_scores(c, j):
                if c >= 2 and j == 0:
                    act.wait_ge(pe_pv, NPB * (c - 1))
                if c == 0 and j == 0:
                    act.wait_ge(v_wlo, 3)
                    act.wait_ge(g_wsq, 2)
                act.wait_ge(pe_s, SU * c + j + 1)
                act.activation(sv_sb[:, c % 2, j * GJ:(j + 1) * GJ, :],
                               s_ps[:, j % 2, 0:GJ * NC].rearrange("p (g n) -> p g n", n=NC),
                               ACT.Copy).then_inc(a_sv, 1)

            def evacuate_y(c, k):
                if c and k == 0:
                    act.wait_ge(v_yr, c)
                act.wait_ge(pe_pv, NPB * c + k + 1)
                act.activation(y_sb[:, :, :, k * 2 * PB:(k + 1) * 2 * PB].rearrange("p h b w -> p w b h"),
                               y_ps[:, k, :].rearrange("p (w b h) -> p w b h", b=HR, h=HEADS),
                               ACT.Copy).then_inc(a_y, 1)

            def exponentials(c):
                act.wait_ge(v_sub, c + 1)
                act.activation(ex[:], ex[:], ACT.Exp, scale=SCALE).then_inc(a_exp, 1)

            for i in range(ITER):
                c0, c1, c2, c3, c4 = range(i, i - 5, -1)
                if 5 <= i < N:
                    act.wait_ge(v_out, 2 * (i - 4))
                if i in (1, 3):
                    act.wait_ge(pe_norm, 2 if i == 1 else 3)

                def l0_out(c, m):
                    evacuate(L0, c, m, x1_sb[:, c % NX1, m])

                def k_out(c, m):
                    if m == 0 and c >= 2:
                        act.wait_ge(a_krhs, 2 * HR * (c - 1))
                    evacuate(K, c, m, kx_sb[:, c % 2, m])

                def o_out(c, m):
                    if m == 0 and c >= 2:
                        act.wait_ge(st_o[c % 2], DMA * (c // 2))
                    evacuate(O, c, m, o_sb[:, c % 2, m].rearrange("p (b j w) -> p j b w", b=HR, j=HR))

                order = [
                    (c0, l0_out, 0), (c1, copy_k, 2), (c0, l0_out, 1), (c1, copy_k, 3), (c0, l0_out, 2),
                    (c2, exponentials), (c0, l0_out, 3), (c0, x1_hi_of, 0),
                    (c4, o_out, 0), (c0, x1_hi_of, 1), (c2, guess_reciprocal), (c4, o_out, 1),
                    (c1, copy_k, 4), (c4, o_out, 2), (c1, copy_k, 5), (c4, o_out, 3), (c1, copy_k, 6),
                    (0 - i, roots_of_k), (1 - i if i else -1, roots_of_o),
                    (c0, k_out, 0), (c1, copy_k, 7), (c0, k_out, 1), (c0, k_out, 2), (c0, k_out, 3),
                    (i + 1, x_hi_of, 0), (c1, evacuate_scores, 0), (i + 1, x_hi_of, 1),
                    (c1, evacuate_scores, 1), (c3, y_hi_of, 0), (c1, evacuate_scores, 2), (c3, y_hi_of, 1),
                    (c1, evacuate_scores, 3), (c2, evacuate_y, 0), (c0, copy_k, 0), (c2, evacuate_y, 1),
                    (c0, copy_k, 1)]
                if i == 0:
                    at = order.index((c0, k_out, 0))
                    order[at:at] = [(1, x_hi_of, 0), (1, x_hi_of, 1)]
                    order = [o for n, o in enumerate(order) if n < at + 2 or o[1] is not x_hi_of]
                if i >= N:
                    order = [(c1, copy_k, p) for p in range(2, 2 * HR)] + [
                        (c2, exponentials), (c4, o_out, 0), (c2, guess_reciprocal), (c4, o_out, 1), (c4, o_out, 2),
                        (c4, o_out, 3), (c3, y_hi_of, 0), (c3, y_hi_of, 1)] + [
                        (c1, evacuate_scores, j) for j in range(SU)] + [(c2, evacuate_y, 0), (c2, evacuate_y, 1)]
                for c, step, *args in order:
                    if 0 <= c < N:
                        step(c, *args)

        @block.vector
        def _(dve):
            def lo_part(l, c, h, out, src, hi, made, raised):
                b = c // PER_BATCH
                dve.wait_ge(made, 2 * c + h + 1)
                for k in range(h * KB // 2, (h + 1) * KB // 2):
                    v = dve.scalar_tensor_tensor(out=out[:, k], in0=src[:, k], scalar=style[l][:, k, b:b + 1],
                                                 in1=hi[:, k], op0=ALU.mult, op1=ALU.subtract)
                v.then_inc(raised, 1)

            def x_lo_of(c, h):
                lo_part(L0, c, h, x_lo, x_sb[:, c % 2], x_hi, a_xhi, v_xlo)

            def x1_lo_of(c, h):
                lo_part(K, c, h, x1_lo, x1_sb[:, c % NX1], x1_hi, a_x1hi, v_x1lo)

            def y_lo_of(c, h):
                lo_part(O, c, h, y_lo[:, c % 2], yr_sb, y_hi[:, c % 2], a_yhi, v_ylo)

            def style_of(l):
                dve.wait_ge(pe_style, l + 1)
                dve.scalar_tensor_tensor(
                    out=style[l][:], in0=y_ps[:, 0, l * KB * B:(l + 1) * KB * B].rearrange("p (k b) -> p k b", b=B),
                    scalar=GAIN[l], in1=affb_sb[l][:].unsqueeze(2).to_broadcast([P, KB, B]),
                    op0=ALU.mult, op1=ALU.add).then_inc(v_style, 1)
                dve.wait_ge(v_style, l + 1)
                dve.tensor_tensor(style_sq[l][:], style[l][:], style[l][:], ALU.mult).then_inc(v_ssq, 1)

            def weights_lo(l):
                dve.wait_ge(a_whi, l + 1)
                dve.tensor_tensor(w_lo[l][:], w_raw[l], w_hi[l][:], ALU.subtract).then_inc(v_wlo, 1)

            def demod_of(l):
                dve.wait_ge(pe_norm, l + 1)
                dve.tensor_scalar(norm[l][:], y_ps[:, 1, l * KB * B:(l + 1) * KB * B]
                                  .rearrange("p (k b) -> p k b", b=B), EPS, None, ALU.add).then_inc(v_norm, 1)
                dve.wait_ge(a_norm, l + 1)
                dve.reciprocal(demod[l][:], norm[l][:]).then_inc(v_demod, 1)

            dve.wait_ge(ld_const[L0], DMA)
            dve.tensor_tensor(w_sq[L0], w_raw[L0], w_raw[L0], ALU.mult).then_inc(v_wsq, 1)
            dve.wait_ge(ld_first, DMA * FIRST)
            style_of(L0)
            weights_lo(L0)
            x_lo_of(0, 0)
            x_lo_of(0, 1)
            demod_of(L0)
            weights_lo(K)
            dve.wait_ge(ld_small, DMA * SMALL)
            dve.tensor_copy(k_rhs[:, HEADS:NC, :], eye[:].unsqueeze(2).to_broadcast([P, HD, TB])).then_inc(v_eye, 1)
            style_of(K)

            def copy_y(c, h):
                tiles = range(h * HR // 2, (h + 1) * HR // 2)
                dve.wait_ge(a_y, NPB * (c + 1))
                if c:
                    dve.wait_ge(a_yhi, 2 * c)
                    dve.wait_ge(v_ylo, 2 * c)
                y_v = y_sb[:, :, :, :].rearrange("p h b w -> p h (b w)")
                for j in tiles:
                    for hr in range(HR):
                        v = dve.tensor_copy(yr_sb[HD * hr:HD * (hr + 1), :, j * TB:(j + 1) * TB],
                                            y_v[HD * j:HD * (j + 1), hr::HR, :])
                if HR - 1 in tiles:
                    v.then_inc(v_yr, 1)

            def make_x1(c, h):
                x1h = x1_sb[:, c % NX1, h * half:(h + 1) * half]
                dve.wait_ge(a_lin, done(L0, c, (h + 1) * half - 1))
                dve.tensor_scalar(x1h, x1h, CLAMP, -CLAMP, ALU.min, ALU.max).then_inc(v_clip, 1)
                dve.wait_ge(v_clip, 2 * c + h + 1)
                dve.tensor_tensor(x1h, x1h, x_sb[:, c % 2, h * half:(h + 1) * half], ALU.add).then_inc(v_x1, 1)

            def maxima(c):
                dve.wait_ge(a_sv, SU * (c + 1))
                dve.tensor_reduce(out=mx[:], in_=sv_sb[:, c % 2, :, 0:HEADS], axis=AX_X,
                                  op=ALU.max).then_inc(v_max, 1)
                dve.wait_ge(v_max, c + 1)
                dve.tensor_copy(mx_hi[:], mx[:]).then_inc(v_mhi, 1)
                dve.wait_ge(v_mhi, c + 1)
                dve.tensor_tensor(mx_lo[:], mx[:], mx_hi[:], ALU.subtract).then_inc(v_mlo, 1)
                dve.wait_ge(v_mlo, c + 1)
                for src, dst in ((mx_hi, md_hi), (mx_lo, md_lo)):
                    v = dve.tensor_tensor(dst[:], src[:].unsqueeze(2).to_broadcast([P, NG, HEADS]),
                                          diag[:].unsqueeze(1).to_broadcast([P, NG, HEADS]), ALU.mult)
                v.then_inc(v_diag, 1)

            def finish(c, h):
                oh = o_sb[:, c % 2, h * half:(h + 1) * half]
                dve.wait_ge(a_lin, done(O, c, (h + 1) * half - 1))
                dve.tensor_tensor(oh, oh, x1_sb[:, c % NX1, h * half:(h + 1) * half], ALU.add).then_inc(v_out, 1)

            half = KB // 2
            def refine_reciprocal(c):
                dve.wait_ge(a_rcp, c + 1)
                dve.tensor_tensor(err[:], rcp[:], cd_ps[:, :].rearrange("p (g h) -> p g h", h=HEADS),
                                  ALU.mult).then_inc(v_err, 1)
                dve.wait_ge(v_err, c + 1)
                dve.scalar_tensor_tensor(out=rcp[:], in0=err[:], scalar=2.0, in1=rcp[:],
                                         op0=ALU.subtract, op1=ALU.mult).then_inc(v_rcp, 1)
                dve.wait_ge(v_rcp, c + 1)
                dve.scalar_tensor_tensor(out=prob[:], in0=rcp[:], scalar=-1.0, in1=ex[:],
                                         op0=ALU.mult, op1=ALU.mult).then_inc(v_prob, 1)

            def spread_probabilities(c):
                dve.wait_ge(v_prob, c + 1)
                dve.wait_ge(pe_pv, NPB * c)
                for t in range(TG):
                    v = dve.tensor_scalar(p_bd[:, :, t, :], prob[:], tok_mask[:, t:t + 1], None, ALU.mult)
                v.then_inc(v_pbd, 1)

            def subtract_maxima(c):
                dve.wait_ge(pe_c, c + 1)
                dve.tensor_tensor(ex[:], sv_sb[:, c % 2, :, 0:HEADS],
                                  cd_ps[:, :].rearrange("p (g h) -> p g h", h=HEADS),
                                  ALU.subtract).then_inc(v_sub, 1)

            def split_exponentials(c):
                dve.wait_ge(a_exp, c + 1)
                dve.tensor_copy(ex_hi[:], ex[:]).then_inc(v_ehi, 1)
                dve.wait_ge(v_ehi, c + 1)
                dve.tensor_tensor(ex_lo[:], ex[:], ex_hi[:], ALU.subtract).then_inc(v_elo, 1)

            def demod_of_k(_):
                demod_of(K)

            def demod_of_o(_):
                style_of(O)
                weights_lo(O)
                demod_of(O)

            for i in range(ITER):
                c0, c1, c2, c3, c4 = range(i, i - 5, -1)
                order = [
                    (c2, subtract_maxima), (c0, make_x1, 0), (c2, split_exponentials), (c0, make_x1, 1),
                    (c3, copy_y, 0), (c0, x1_lo_of, 0), (c0, x1_lo_of, 1),
                    (0 - i, demod_of_k), (1 - i if i else -1, demod_of_o),
                    (c2, refine_reciprocal), (c4, finish, 0), (c2, spread_probabilities), (c4, finish, 1),
                    (c3, copy_y, 1), (i + 1, x_lo_of, 0), (i + 1, x_lo_of, 1),
                    (c3, y_lo_of, 0), (c3, y_lo_of, 1), (c1, maxima)]
                if i >= N:
                    order = [(c2, subtract_maxima), (c2, split_exponentials), (c3, copy_y, 0),
                             (c2, refine_reciprocal), (c2, spread_probabilities), (c3, copy_y, 1),
                             (c4, finish, 0), (c4, finish, 1), (c3, y_lo_of, 0), (c3, y_lo_of, 1), (c1, maxima)]
                for c, step, *args in order:
                    if 0 <= c < N:
                        step(c, *args)


FIRST, SMALL = 3, 11

_LAYERS = (("L0_cond_weight", "L0_cond_affine_w", "L0_cond_affine_b", "L0_cond_bias"),
           ("L1_cond_k_w", "L1_cond_k_aff_w", "L1_cond_k_aff_b", "L1_cond_k_b"),
           ("L1_cond_o_w", "L1_cond_o_aff_w", "L1_cond_o_aff_b", "L1_cond_o_b"))


def kernel(**inputs):
    import numpy as np
    import concourse.bacc as bacc
    from concourse.bass_utils import run_bass_kernel_spmd

    x = np.asarray(inputs["x"])
    B, L, F = x.shape
    part = np.arange(P)
    cols = lambda v: np.ascontiguousarray(np.asarray(v).reshape(F // P, P).T)
    turned = lambda a: np.ascontiguousarray(np.asarray(a).T)
    arrays = {"xT": turned(x.reshape(B * L, F)), "condT": turned(inputs["cond_512"])}
    for l, (w, aw, ab, b) in enumerate(_LAYERS):
        arrays[f"wT{l}"], arrays[f"affT{l}"] = turned(inputs[w]), turned(inputs[aw])
        arrays[f"aff_b{l}"], arrays[f"lin_b{l}"] = cols(inputs[ab]), cols(inputs[b])
    HD = F // HEADS
    arrays["block_ones"] = (part[:, None] // HEADS == part[None, :] // HEADS).astype(np.float32)
    arrays["token_mask"] = (part[:, None] // HEADS == np.arange(P // HEADS)[None, :]).astype(np.float32)
    arrays["head_diag"] = (part[:, None] % HEADS == np.arange(HEADS)[None, :]).astype(np.float32)
    arrays["dim_eye"] = (part[:, None] % HD == np.arange(HD)[None, :]).astype(np.float32)

    nc = bacc.Bacc("TRN2", target_bir_lowering=False, num_devices=1)
    d = {n: nc.dram_tensor(n, a.shape, mybir.dt.from_np(a.dtype), kind="ExternalInput").ap() for n, a in arrays.items()}
    outT = nc.dram_tensor("outT", (F, B * L), F32, kind="ExternalOutput").ap()
    three = lambda n: [d[f"{n}{l}"] for l in range(3)]
    build(nc, d["xT"], d["condT"], three("wT"), three("affT"), three("aff_b"), three("lin_b"),
          d["block_ones"], d["token_mask"], d["head_diag"], d["dim_eye"], outT)
    r = run_bass_kernel_spmd(nc, [arrays], core_ids=[0])
    return np.ascontiguousarray(r.results[0]["outT"].T).reshape(B, L, F)
```

```python
from contextlib import ExitStack

import concourse.bass as bass
from concourse import mybir

F32 = mybir.dt.float32
F32R = mybir.dt.float32r
ALU = mybir.AluOpType
ACT = mybir.ActivationFunctionType
AX_X = mybir.AxisListType.X

P = 128
HEADS = 16
EPS = 1e-8
CLAMP = 256.0
DMA = 16


def build(nc, xT, condT, wT, affT, aff_b, lin_b, block_ones, token_mask, head_diag, dim_eye, outT):
    F, NT = xT.shape
    SD, B = condT.shape
    HD = F // HEADS
    KB = F // P
    SB = SD // P
    HR = P // HD
    T = 256
    N = NT // T
    PER_BATCH = NT // B // T
    TB = T // HR
    TG = P // HEADS
    NG = T // TG
    GJ = NG // HR
    NC = HEADS + HD
    SU = NG // GJ
    PB = 512 // P
    NPB = GJ // PB
    W = TB // HR
    DEPTH = 4
    NX1 = DEPTH + 1
    NLB = 3
    GAIN = (float(SD) ** -0.5, 1.0, 1.0)
    SCALE = float(HD) ** -0.5
    L0, K, O = range(3)
    assert HR == 4 and TG == 8 and GJ * NC <= 512 and NG * HEADS == 512 and W == 2 * GJ

    xT_v = xT.rearrange("(k p) t -> p k t", p=P)
    outT_v = outT.rearrange("(k p) t -> p k t", p=P)

    with ExitStack() as ctx:
        def sb(name, shape, dt=F32):
            return ctx.enter_context(nc.sbuf_tensor(name, [P] + shape, dt))

        def ps(name, shape):
            return ctx.enter_context(nc.psum_tensor(name, [P] + shape, F32))

        def sem(name):
            return ctx.enter_context(nc.semaphore(name))

        w_hi = [sb(f"w_hi{l}", [KB, F], F32R) for l in range(3)]
        w_lo = [sb(f"w_lo{l}", [KB, F], F32R) for l in range(3)]
        style = [sb(f"style{l}", [KB, B]) for l in range(3)]
        style_sq = [sb(f"style_sq{l}", [KB, B]) for l in range(3)]
        demod = [sb(f"demod{l}", [KB, B]) for l in range(3)]
        norm = [sb(f"norm{l}", [KB, B]) for l in range(3)]
        affb_sb = [sb(f"affb{l}", [KB]) for l in range(3)]
        bias_sb = [sb(f"bias{l}", [KB]) for l in range(3)]
        cond_sb = sb("cond", [SB, B])
        eps_sb = sb("eps", [1])
        ones_f = sb("ones_f", [P])
        ones_r = sb("ones_r", [P], F32R)
        tok_mask = sb("tok_mask", [TG])
        diag = sb("diag", [HEADS])
        eye = sb("eye", [HD])
        x_sb = sb("x", [2, KB, T])
        x1_sb = sb("x1", [NX1, KB, T])
        x_hi, x_lo = sb("x_hi", [KB, T], F32R), sb("x_lo", [KB, T], F32R)
        x1_hi, x1_lo = sb("x1_hi", [KB, T], F32R), sb("x1_lo", [KB, T], F32R)
        kx_sb = sb("kx", [2, KB, T])
        k_rhs = sb("k_rhs", [NC, TB])
        k_bd = sb("k_bd", [HR * HEADS, TB])
        sv_sb = sb("sv", [2, NG, NC])
        mx = sb("mx", [NG])
        mx_hi, mx_lo = sb("mx_hi", [NG], F32R), sb("mx_lo", [NG], F32R)
        md_hi, md_lo = sb("md_hi", [NG, HEADS], F32R), sb("md_lo", [NG, HEADS], F32R)
        ex = sb("ex", [NG, HEADS])
        ex_hi, ex_lo = sb("ex_hi", [NG, HEADS], F32R), sb("ex_lo", [NG, HEADS], F32R)
        rcp = sb("rcp", [NG, HEADS])
        err = sb("err", [NG, HEADS])
        prob = sb("prob", [NG, HEADS])
        p_bd = sb("p_bd", [NG, TG, HEADS])
        y_sb = sb("y", [HEADS, HR, W])
        yr_sb = sb("yr", [KB, T])
        y_hi, y_lo = sb("y_hi", [2, KB, T], F32R), sb("y_lo", [2, KB, T], F32R)
        o_sb = sb("o", [2, KB, T])
        def halves(t, a, b, n=2):
            names = [f"d{d}" for d in range(len(t.shape) - 1)]
            flat = t.rearrange(f"p {' '.join(names)} -> p ({' '.join(names)})")
            return [flat[:, h * a * b:(h + 1) * a * b].rearrange("p (a b) -> p a b", a=a) for h in range(n)]

        aff_v = [halves(t, SB, F, 1)[0] for t in (o_sb[:, 0], y_sb[:, :, :, :], yr_sb[:, :, :])]
        w_raw = halves(p_bd[:, :, :, :], KB, F) + halves(sv_sb[:, :, :, :], KB, F, 1)
        w_sq = halves(k_bd[:, :, :], KB, F, 1) + halves(x1_sb[:, 1:NX1], KB, F)

        lin_ps = ps("lin_ps", [NLB, 512])
        s_ps = ps("s_ps", [2, 512])
        cd_ps = ps("cd_ps", [512])
        y_ps = ps("y_ps", [NPB, 512])

        ld_w = [[sem(f"ld_w{l}_{h}") for h in range(2)] for l in range(3)]
        ld_first, ld_small = sem("ld_first"), sem("ld_small")
        ld_x = [sem(f"ld_x{i}") for i in range(2)]
        ld_kbd = sem("ld_kbd")
        st_o = [sem(f"st_o{i}") for i in range(2)]
        g_eps, g_zero = sem("g_eps"), sem("g_zero")
        v_eye = sem("v_eye")
        pe_style, v_style = sem("pe_style"), sem("v_style")
        v_ssq, a_wsq, g_wsq = sem("v_ssq"), sem("a_wsq"), sem("g_wsq")
        pe_norm, a_norm, v_demod = sem("pe_norm"), sem("a_norm"), sem("v_demod")
        a_whi, v_wlo, a_ones = sem("a_whi"), sem("v_wlo"), sem("a_ones")
        pe_lin, a_lin = sem("pe_lin"), sem("a_lin")
        a_xhi, v_xlo = sem("a_xhi"), sem("v_xlo")
        v_clip, v_x1 = sem("v_clip"), sem("v_x1")
        a_x1hi, v_x1lo = sem("a_x1hi"), sem("v_x1lo")
        a_krhs, v_krhs = sem("a_krhs"), sem("v_krhs")
        pe_s, a_sv = sem("pe_s"), sem("a_sv")
        v_max, v_mhi, v_mlo, v_diag = sem("v_max"), sem("v_mhi"), sem("v_mlo"), sem("v_diag")
        pe_c, v_sub, a_exp = sem("pe_c"), sem("v_sub"), sem("a_exp")
        v_ehi, v_elo, pe_d = sem("v_ehi"), sem("v_elo"), sem("pe_d")
        a_ln, a_rcp, v_err, v_rcp = sem("a_ln"), sem("a_rcp"), sem("v_err"), sem("v_rcp")
        v_prob, v_pbd, a_pbd = sem("v_prob"), sem("v_pbd"), sem("a_pbd")
        pe_pv, a_y, v_yr, a_yr = sem("pe_pv"), sem("a_y"), sem("v_yr"), sem("a_yr")
        a_yhi, v_ylo = sem("a_yhi"), sem("v_ylo")
        v_out = sem("v_out")

        def blocks(l, c, ms=range(KB)):
            return [("lin", l, c, m) for m in ms]

        def score_units(c, js=range(SU)):
            return [("scores", c, j) for j in js]

        def one(step, c):
            return [(step, c)]

        def norms_of(l, ms):
            return [("norms", l, m) for m in ms]

        last = N - 1

        def pe_steps(i):
            return (blocks(L0, i, [0, 1]) + one("max", i - 2) + blocks(L0, i, [2, 3])
                    + blocks(O, i - 4, [0, 1]) + one("sum", i - 2) + blocks(O, i - 4, [2, 3])
                    + blocks(K, i) + score_units(i - 1) + one("pv", i - 2))

        SHARED_K = (0, 1, 2, last)
        SHARED_Y, SHARED_P = N - 3, N - 2

        def k_moved(c):
            shared = len([s for s in SHARED_K if s <= c])
            return 2 * HR * (c + 1) - HR * shared, HR * shared

        pe_program = (
            one("styles", L0) + blocks(L0, 0, [0, 1]) + norms_of(L0, [0]) + blocks(L0, 0, [2])
            + norms_of(L0, [1, 2, 3]) + blocks(L0, 0, [3]) + one("styles", K) + blocks(L0, 1, [0])
            + norms_of(K, [0, 1]) + blocks(L0, 1, [1]) + norms_of(K, [2, 3]) + blocks(L0, 1, [2]) + one("styles", O)
            + blocks(L0, 1, [3]) + norms_of(O, [0, 1, 2]) + blocks(K, 0, [0, 1]) + norms_of(O, [3])
            + blocks(K, 0, [2, 3]) + blocks(L0, 2) + blocks(K, 1) + score_units(0) + blocks(L0, 3, [0, 1, 2])
            + one("max", 0) + blocks(L0, 3, [3]) + one("sum", 0) + blocks(K, 2) + score_units(1) + one("pv", 0)
            + blocks(K, 3, [0, 1]) + one("max", 1) + blocks(K, 3, [2]) + blocks(L0, 4, [0, 1]) + blocks(K, 3, [3])
            + one("sum", 1) + score_units(2, [0, 1]) + blocks(L0, 4, [2]) + score_units(2, [2, 3]) + one("pv", 1)
            + blocks(L0, 4, [3]) + one("max", 2) + blocks(O, 0, [0, 1, 2]) + one("sum", 2) + blocks(O, 0, [3])
            + blocks(K, 4) + score_units(3) + one("pv", 2))
        pe_program += [step for i in range(DEPTH + 1, last) for step in pe_steps(i)]
        pe_program += (
            blocks(L0, last, [0, 1]) + one("max", last - 2) + blocks(L0, last, [2, 3]) + blocks(O, last - 4, [0])
            + one("sum", last - 2) + blocks(O, last - 4, [1]) + blocks(K, last) + score_units(last - 1)
            + one("pv", last - 2) + blocks(O, last - 4, [2]) + one("max", last - 1) + blocks(O, last - 4, [3])
            + blocks(O, last - 3, [0, 1]) + score_units(last, [0, 1]) + one("sum", last - 1)
            + score_units(last, [2]) + blocks(O, last - 3, [2, 3]) + score_units(last, [3])
            + blocks(O, last - 2, [0]) + one("pv", last - 1) + one("max", last) + blocks(O, last - 2, [1, 2])
            + one("sum", last) + blocks(O, last - 2, [3]) + blocks(O, last - 1, [0, 1]) + one("pv", last)
            + blocks(O, last - 1, [2, 3]) + blocks(O, last))
        block_no = {}
        for step in pe_program:
            if step[0] == "lin":
                block_no[step[1:]] = len(block_no)

        def done(l, c, m):
            return block_no[(l, c, m)] + 1

        def heads_to_partitions(copy, j):
            y_v = y_sb[:, :, :, :].rearrange("p h b w -> p h (b w)")
            for hr in range(HR):
                inst = copy(yr_sb[HD * hr:HD * (hr + 1), :, j * TB:(j + 1) * TB], y_v[HD * j:HD * (j + 1), hr::HR, :])
            return inst

        def kx_to_block(copy, c, part):
            tb, h = part // 2, part % 2
            for hr in range(h * HR // 2, (h + 1) * HR // 2):
                inst = copy(k_rhs[HD * tb:HD * (tb + 1), hr:HEADS:HR, :],
                            kx_sb[HD * hr:HD * (hr + 1), c % 2, :, tb * TB:(tb + 1) * TB])
            return inst

        block = ctx.enter_context(nc.Block())

        @block.sync
        def _(sp):
            def load_x(c):
                if c >= 2:
                    sp.wait_ge(v_x1, 2 * (c - 1))
                sp.dma_start(x_sb[:, c % 2], xT_v[:, :, c * T:(c + 1) * T]).then_inc(ld_x[c % 2], DMA)

            def load_affine(l, landed):
                sp.dma_start(aff_v[l], affT[l].rearrange("(s p) f -> p s f", p=P)).then_inc(landed, DMA)
                sp.dma_start(affb_sb[l][:], aff_b[l]).then_inc(landed, DMA)

            def load_weights(l, h):
                ks = slice(h * KB // 2, (h + 1) * KB // 2)
                sp.dma_start(w_raw[l][:, ks], wT[l].rearrange("(k p) f -> p k f", p=P)[:, ks]).then_inc(
                    ld_w[l][h], DMA)

            def spread_k(c):
                if c == 0:
                    sp.wait_ge(g_zero, 1)
                else:
                    sp.wait_ge(pe_s, SU * c)
                for tb in range(HR):
                    by_act, by_dve = k_moved(c)
                    if c in SHARED_K and tb >= HR // 2:
                        sp.wait_ge(v_krhs, by_dve - 2 * (HR - tb - 1))
                    else:
                        sp.wait_ge(a_krhs, by_act - 2 * ((HR // 2 if c in SHARED_K else HR) - tb - 1))
                    sp.dma_start(k_bd[HD * tb:HD * (tb + 1), tb * HEADS:(tb + 1) * HEADS, :],
                                 k_rhs[HD * tb:HD * (tb + 1), 0:HEADS, :]).then_inc(ld_kbd, DMA)

            def store(c, h, parts):
                ks = slice(h * KB // parts, (h + 1) * KB // parts)
                sp.wait_ge(v_out, 2 * c + 2 * (h + 1) // parts)
                sp.dma_start(outT_v[:, ks, c * T:(c + 1) * T], o_sb[:, c % 2, ks]).then_inc(st_o[c % 2], DMA)

            sp.dma_start(cond_sb[:], condT.rearrange("(s p) b -> p s b", p=P)).then_inc(ld_first, DMA)
            load_affine(L0, ld_first)
            load_x(0)
            load_weights(L0, 0)
            load_weights(L0, 1)
            load_affine(K, ld_small)
            load_weights(K, 0)
            load_weights(K, 1)
            for l in range(3):
                sp.dma_start(bias_sb[l][:], lin_b[l]).then_inc(ld_small, DMA)
            load_affine(O, ld_small)
            for src, dst in [(block_ones, ones_f), (token_mask, tok_mask), (head_diag, diag), (dim_eye, eye)]:
                sp.dma_start(dst[:], src).then_inc(ld_small, DMA)
            load_weights(O, 0)
            load_weights(O, 1)
            load_x(1)

            for i in range(N):
                if i < 3:
                    load_x(i + 2)
                if i >= 1:
                    spread_k(i - 1)
                if 3 <= i < N - 2:
                    load_x(i + 2)
                if DEPTH <= i < last:
                    store(i - 4, 0, 1)
            spread_k(last)
            for c in range(last - DEPTH, last):
                store(c, 0, 1)
            for h in range(2):
                store(last, h, 2)
            for b in range(2):
                sp.wait_ge(st_o[b], DMA * (len(range(b, N, 2)) + (b == last % 2)))

        @block.gpsimd
        def _(pool):
            pool.memset(eps_sb[:, :], EPS).then_inc(g_eps, 1)
            for l in (K, O):
                for h in range(2):
                    pool.wait_ge(ld_w[l][h], DMA)
                pool.tensor_tensor(w_sq[l], w_raw[l], w_raw[l], ALU.mult).then_inc(g_wsq, 1)
            pool.wait_ge(pe_norm, 1)
            pool.memset(k_bd[:, :, :], 0.0).then_inc(g_zero, 1)

        @block.tensor
        def _(pe):
            operands = {L0: (x_hi, x_lo), K: (x1_hi, x1_lo)}
            split = {L0: (a_xhi, v_xlo), K: (a_x1hi, v_x1lo), O: (a_yhi, v_ylo)}

            def linear(l, c, m):
                n = block_no[(l, c, m)]
                if n >= NLB:
                    pe.wait_ge(a_lin, n - NLB + 1)
                hi, lo = (y_hi[:, c % 2], y_lo[:, c % 2]) if l == O else operands[l]
                passes = [(k, w, r) for k in range(KB)
                          for w, r in ((w_hi[l], hi), (w_hi[l], lo), (w_lo[l], hi))]
                for q, (k, w, r) in enumerate(passes):
                    if m == 0 and q in (0, len(passes) // 2):
                        h = int(q > 0)
                        pe.wait_ge(split[l][0], 2 * c + h + 1)
                        pe.wait_ge(split[l][1], 2 * c + h + 1)
                        if c == 0:
                            pe.wait_ge(a_whi, 2 * l + h + 1)
                            pe.wait_ge(v_wlo, 2 * l + h + 1)
                    mm = pe.matmul(lin_ps[:, n % NLB, 0:T], w[:, k, m * P:(m + 1) * P], r[:, k, :],
                                   start=(q == 0), stop=(q == len(passes) - 1))
                mm.then_inc(pe_lin, 1)

            def styles(l):
                pe.wait_ge(ld_first, DMA * FIRST)
                if l:
                    pe.wait_ge(ld_small, DMA * SMALL)
                    pe.wait_ge(v_style, l)
                for m in range(KB):
                    for s in range(SB):
                        mm = pe.matmul(y_ps[:, 0, (l * KB + m) * B:(l * KB + m + 1) * B],
                                       aff_v[l][:, s, m * P:(m + 1) * P], cond_sb[:, s, :],
                                       start=(s == 0), stop=(s == SB - 1))
                mm.then_inc(pe_style, 1)

            def norms(l, m):
                if m == 0:
                    pe.wait_ge(v_ssq, l + 1)
                    pe.wait_ge(*((a_wsq, 1) if l == L0 else (g_wsq, l)))
                if l:
                    pe.wait_ge(a_norm, l)
                for k in range(KB):
                    mm = pe.matmul(y_ps[:, 1, (l * KB + m) * B:(l * KB + m + 1) * B],
                                   w_sq[l][:, k, m * P:(m + 1) * P], style_sq[l][:, k, :],
                                   start=(k == 0), stop=(k == KB - 1))
                if m == KB - 1:
                    mm.then_inc(pe_norm, 1)

            def scores(c, j):
                if j == 0:
                    pe.wait_ge(ld_kbd, DMA * HR * (c + 1))
                    if c == 0:
                        pe.wait_ge(v_eye, 1)
                if SU * c + j >= 2:
                    pe.wait_ge(a_sv, SU * c + j - 1)
                for q in range(GJ):
                    for u in range(2):
                        g = j * W + 2 * q + u
                        mm = pe.matmul(s_ps[64 * u:64 * u + 64, j % 2, q * NC:(q + 1) * NC],
                                       k_bd[:, :, g], k_rhs[:, :, g], start=True, stop=True)
                mm.then_inc(pe_s, 1)

            def over_token(c, ready, hi, lo, raised):
                pe.wait_ge(ready, c + 1)
                for r in (hi, lo):
                    mm = pe.matmul(cd_ps[:, :], ones_r[:, :], r[:, :, :].rearrange("p g h -> p (g h)"),
                                   start=(r is hi), stop=(r is lo))
                mm.then_inc(raised, 1)

            def pv(c):
                pe.wait_ge(v_pbd, c + 1)
                if c >= SHARED_P:
                    pe.wait_ge(a_pbd, c - SHARED_P + 1)
                if c == 0:
                    pe.wait_ge(a_norm, 3)
                for q in range(GJ):
                    if q % PB == 0 and c:
                        pe.wait_ge(a_y, NPB * (c - 1) + q // PB + 1)
                    for j in range(HR):
                        grp = j * GJ + q
                        mm = pe.matmul(y_ps[HD * j:HD * (j + 1), q // PB, (q % PB) * P:(q % PB + 1) * P],
                                       sv_sb[:, c % 2, grp, HEADS:NC],
                                       p_bd[:, grp].rearrange("p t h -> p (t h)"), start=True, stop=True)
                    if q % PB == PB - 1:
                        mm.then_inc(pe_pv, 1)

            def maxima_over_token(c):
                if c == 0:
                    pe.wait_ge(a_ones, 1)
                else:
                    pe.wait_ge(v_err, c)
                over_token(c, v_diag, md_hi, md_lo, pe_c)

            def sums_over_token(c):
                over_token(c, v_elo, ex_hi, ex_lo, pe_d)

            stages = {"lin": linear, "styles": styles, "norms": norms, "scores": scores, "pv": pv,
                      "max": maxima_over_token, "sum": sums_over_token}
            for stage, *args in pe_program:
                stages[stage](*args)

        @block.scalar
        def _(act):
            evacuated = []

            def evacuate(l, c, m, out):
                evacuated.append((l, c, m))
                assert done(l, c, m) == len(evacuated)
                act.wait_ge(pe_lin, done(l, c, m))
                b = c // PER_BATCH
                if c == 0 and m == 0:
                    act.wait_ge(v_demod, l + 1)
                src = lin_ps[:, block_no[(l, c, m)] % NLB, 0:T]
                if l == O:
                    src = src.rearrange("p (j b w) -> p j b w", j=HR, b=HR)
                act.activation(out, src, ACT.Identity, bias=bias_sb[l][:, m:m + 1],
                               scale=demod[l][:, m, b:b + 1]).then_inc(a_lin, 1)

            def hi_part(l, c, h, out, src, raised):
                b = c // PER_BATCH
                if c == 0:
                    act.wait_ge(v_style, l + 1)
                for k in range(h * KB // 2, (h + 1) * KB // 2):
                    a = act.activation(out[:, k], src[:, k], ACT.Copy, scale=style[l][:, k, b:b + 1])
                a.then_inc(raised, 1)

            def x_hi_of(c, h):
                act.wait_ge(ld_x[c % 2], DMA * (c // 2 + 1))
                if c:
                    act.wait_ge(pe_lin, done(L0, c - 1, KB - 1))
                hi_part(L0, c, h, x_hi, x_sb[:, c % 2], a_xhi)

            def weights_hi(l, h):
                ks = slice(h * KB // 2, (h + 1) * KB // 2)
                act.wait_ge(ld_w[l][h], DMA)
                act.activation(w_hi[l][:, ks], w_raw[l][:, ks], ACT.Copy).then_inc(a_whi, 1)

            def copy(out, src):
                return act.activation(out, src, ACT.Copy)

            def ones_rounded(_):
                act.activation(ones_r[:], ones_f[:], ACT.Copy).then_inc(a_ones, 1)

            def roots(l):
                act.wait_ge(pe_norm, l + 1)
                act.activation(norm[l][:], y_ps[:, 1, l * KB * B:(l + 1) * KB * B].rearrange("p (k b) -> p k b", b=B),
                               ACT.Sqrt, bias=eps_sb[:, 0:1]).then_inc(a_norm, 1)
                if l == O:
                    act.preload_act_table_set("natural_log_exp_and_others")

            def copy_k(c, part):
                if part == 0:
                    act.wait_ge(a_lin, done(K, c, KB - 1))
                    if c:
                        act.wait_ge(pe_s, SU * c)
                kx_to_block(copy, c, part).then_inc(a_krhs, 1)

            act.preload_act_table_set("sqrt_and_others")
            x_hi_of(0, 0)
            weights_hi(L0, 0)
            x_hi_of(0, 1)
            weights_hi(L0, 1)
            act.activation(w_sq[L0], w_raw[L0], ACT.Square).then_inc(a_wsq, 1)
            weights_hi(K, 0)
            weights_hi(K, 1)
            act.wait_ge(g_eps, 1)
            roots(L0)
            act.wait_ge(ld_small, DMA * SMALL)

            def guess_reciprocal(c):
                act.wait_ge(pe_d, c + 1)
                act.activation(rcp[:], cd_ps[:, :].rearrange("p (g h) -> p g h", h=HEADS), ACT.Ln).then_inc(a_ln, 1)
                act.wait_ge(a_ln, c + 1)
                act.activation(rcp[:], rcp[:], ACT.Exp, scale=-1.0).then_inc(a_rcp, 1)

            def x1_hi_of(c, h):
                if c and h == 0:
                    act.wait_ge(pe_lin, done(K, c - 1, KB - 1))
                act.wait_ge(v_x1, 2 * c + h + 1)
                hi_part(K, c, h, x1_hi, x1_sb[:, c % NX1], a_x1hi)

            def y_hi_of(c, h):
                act.wait_ge(v_yr, c + 1)
                if c >= SHARED_Y:
                    act.wait_ge(a_yr, c - SHARED_Y + 1)
                if c >= 2:
                    act.wait_ge(pe_lin, done(O, c - 2, KB - 1))
                hi_part(O, c, h, y_hi[:, c % 2], yr_sb, a_yhi)

            def evacuate_scores(c, j):
                if c >= 2 and j == 0:
                    act.wait_ge(pe_pv, NPB * (c - 1))
                if c == 0 and j == 0:
                    act.wait_ge(v_wlo, 6)
                    act.wait_ge(g_wsq, 2)
                act.wait_ge(pe_s, SU * c + j + 1)
                act.activation(sv_sb[:, c % 2, j * GJ:(j + 1) * GJ, :],
                               s_ps[:, j % 2, 0:GJ * NC].rearrange("p (g n) -> p g n", n=NC),
                               ACT.Copy).then_inc(a_sv, 1)

            def evacuate_y(c, k):
                if c and k == 0:
                    act.wait_ge(v_yr, c)
                    if c > SHARED_Y:
                        act.wait_ge(a_yr, c - SHARED_Y)
                act.wait_ge(pe_pv, NPB * c + k + 1)
                act.activation(y_sb[:, :, :, k * 2 * PB:(k + 1) * 2 * PB].rearrange("p h b w -> p w b h"),
                               y_ps[:, k, :].rearrange("p (w b h) -> p w b h", b=HR, h=HEADS),
                               ACT.Copy).then_inc(a_y, 1)

            def exponentials(c):
                act.wait_ge(v_sub, c + 1)
                act.activation(ex[:], ex[:], ACT.Exp, scale=SCALE).then_inc(a_exp, 1)

            def spread_some(c):
                act.wait_ge(v_prob, c + 1)
                act.wait_ge(pe_pv, NPB * c)
                for t in range(TG // 2, TG):
                    a = act.activation(p_bd[:, :, t, :], prob[:], ACT.Copy, scale=tok_mask[:, t:t + 1])
                a.then_inc(a_pbd, 1)

            def copy_some_y(c):
                act.wait_ge(a_y, NPB * (c + 1))
                act.wait_ge(a_yhi, 2 * c)
                act.wait_ge(v_ylo, 2 * c)
                for j in range(HR // 2, HR):
                    a = heads_to_partitions(copy, j)
                a.then_inc(a_yr, 1)

            def l0_out(c, m):
                if m == 0 and c >= NX1:
                    act.wait_ge(v_out, 2 * (c - DEPTH))
                if m == 0 and c in (1, 3):
                    act.wait_ge(pe_norm, 2 if c == 1 else 3)
                evacuate(L0, c, m, x1_sb[:, c % NX1, m])

            def k_out(c, m):
                if m == 0 and c >= 2:
                    act.wait_ge(a_krhs, k_moved(c - 2)[0])
                    act.wait_ge(v_krhs, k_moved(c - 2)[1])
                evacuate(K, c, m, kx_sb[:, c % 2, m])

            def o_out(c, m):
                if m == 0 and c >= 2:
                    act.wait_ge(st_o[c % 2], DMA * (c // 2))
                evacuate(O, c, m, o_sb[:, c % 2, m].rearrange("p (b j w) -> p j b w", b=HR, j=HR))

            def act_steps(i):
                c0, c1, c2, c3, c4 = range(i, i - 5, -1)
                return [
                    (c0, l0_out, 0), (c1, copy_k, 2), (c1, copy_k, 3), (c0, l0_out, 1), (c1, copy_k, 4),
                    (c0, l0_out, 2), (c2, exponentials), (c0, l0_out, 3), (c1, copy_k, 5), (c0, x1_hi_of, 0),
                    (c4, o_out, 0), (c0, x1_hi_of, 1), (c4, o_out, 1), (c2, guess_reciprocal),
                    (c1, copy_k, 6), (c4, o_out, 2), (c1, copy_k, 7), (c4, o_out, 3),
                    (c0, k_out, 0), (c0, k_out, 1), (c0, k_out, 2), (c0, k_out, 3),
                    (i + 1, x_hi_of, 0), (c1, evacuate_scores, 0), (i + 1, x_hi_of, 1),
                    (c1, evacuate_scores, 1), (c3, y_hi_of, 0), (c1, evacuate_scores, 2), (c3, y_hi_of, 1),
                    (c1, evacuate_scores, 3), (c2, evacuate_y, 0), (c0, copy_k, 0), (c2, evacuate_y, 1),
                    (c0, copy_k, 1)]

            act_head = [
                (0, l0_out, 0), (0, ones_rounded), (0, l0_out, 1), (1, x_hi_of, 0), (1, x_hi_of, 1), (0, l0_out, 2),
                (0, l0_out, 3), (1, l0_out, 0), (0, x1_hi_of, 0), (0, x1_hi_of, 1), (O, weights_hi, 0), (K, roots),
                (1, l0_out, 1), (1, l0_out, 2), (1, l0_out, 3), (O, weights_hi, 1), (2, x_hi_of, 0), (0, k_out, 0),
                (2, x_hi_of, 1), (O, roots), (0, k_out, 1), (0, k_out, 2), (0, k_out, 3), (0, copy_k, 0),
                (0, copy_k, 1), (1, x1_hi_of, 0), (2, l0_out, 0), (0, copy_k, 2), (0, copy_k, 3), (1, x1_hi_of, 1),
                (2, l0_out, 1), (2, l0_out, 2), (2, l0_out, 3), (1, k_out, 0), (1, k_out, 1), (3, x_hi_of, 0),
                (3, x_hi_of, 1), (2, x1_hi_of, 0), (1, k_out, 2), (0, evacuate_scores, 0), (1, k_out, 3),
                (2, x1_hi_of, 1), (0, evacuate_scores, 1), (0, evacuate_scores, 2), (1, copy_k, 0),
                (0, evacuate_scores, 3), (1, copy_k, 1), (3, l0_out, 0), (3, l0_out, 1), (0, exponentials),
                (1, copy_k, 2), (3, l0_out, 2), (3, l0_out, 3), (4, x_hi_of, 0), (1, copy_k, 3),
                (0, guess_reciprocal), (2, k_out, 0), (2, k_out, 1), (4, x_hi_of, 1), (3, x1_hi_of, 0),
                (2, k_out, 2), (1, evacuate_scores, 0), (2, k_out, 3), (1, evacuate_scores, 1), (3, x1_hi_of, 1),
                (1, evacuate_scores, 2), (1, evacuate_scores, 3), (2, copy_k, 0), (0, evacuate_y, 0), (2, copy_k, 1),
                (0, evacuate_y, 1), (2, copy_k, 2), (2, copy_k, 3), (3, k_out, 0), (1, exponentials), (3, k_out, 1),
                (3, k_out, 2), (4, l0_out, 0), (4, l0_out, 1), (3, k_out, 3), (1, guess_reciprocal),
                (2, evacuate_scores, 0), (2, evacuate_scores, 1), (2, evacuate_scores, 2), (0, y_hi_of, 0),
                (2, evacuate_scores, 3), (0, y_hi_of, 1), (3, copy_k, 0), (4, l0_out, 2), (3, copy_k, 1),
                (1, evacuate_y, 0), (1, evacuate_y, 1), (3, copy_k, 2), (3, copy_k, 3), (4, x1_hi_of, 0),
                (4, l0_out, 3), (3, copy_k, 4), (2, exponentials), (4, x1_hi_of, 1), (3, copy_k, 5), (0, o_out, 0),
                (0, o_out, 1), (3, copy_k, 6), (2, guess_reciprocal), (0, o_out, 2), (0, o_out, 3), (3, copy_k, 7),
                (5, x_hi_of, 0), (4, k_out, 0), (1, y_hi_of, 0), (1, y_hi_of, 1), (3, evacuate_scores, 0),
                (3, evacuate_scores, 1), (4, k_out, 1), (5, x_hi_of, 1), (4, k_out, 2), (4, k_out, 3),
                (3, evacuate_scores, 2), (3, evacuate_scores, 3), (4, copy_k, 0), (4, copy_k, 1), (2, evacuate_y, 0),
                (2, evacuate_y, 1)]
            act_tail = [
                (last - 1, copy_k, 2), (last - 1, copy_k, 3), (last, l0_out, 0), (last, l0_out, 1),
                (last - 2, exponentials), (last - 1, copy_k, 4), (last, l0_out, 2), (last, l0_out, 3),
                (last - 1, copy_k, 5), (last, x1_hi_of, 0), (last - 4, o_out, 0), (last, x1_hi_of, 1),
                (last - 1, copy_k, 6), (last - 1, copy_k, 7), (last - 2, guess_reciprocal), (last - 4, o_out, 1),
                (last, k_out, 0), (last, k_out, 1), (last, k_out, 2), (last - 1, evacuate_scores, 0),
                (last, k_out, 3), (last - 1, evacuate_scores, 1), (last - 3, y_hi_of, 0), (last - 3, y_hi_of, 1),
                (last - 1, evacuate_scores, 2), (last - 1, evacuate_scores, 3), (last - 2, evacuate_y, 0),
                (last, copy_k, 0), (last, copy_k, 1), (last, copy_k, 2), (last - 4, o_out, 2), (last, copy_k, 3),
                (last - 2, evacuate_y, 1), (last - 2, copy_some_y), (last - 1, exponentials), (last - 4, o_out, 3),
                (last - 3, o_out, 0), (last - 3, o_out, 1), (last - 2, y_hi_of, 0), (last, evacuate_scores, 0),
                (last - 1, guess_reciprocal), (last - 2, y_hi_of, 1), (last, evacuate_scores, 1),
                (last, evacuate_scores, 2), (last - 1, spread_some), (last, evacuate_scores, 3),
                (last - 3, o_out, 2), (last - 3, o_out, 3), (last - 1, evacuate_y, 0), (last - 2, o_out, 0),
                (last - 1, evacuate_y, 1), (last - 1, copy_some_y), (last, exponentials), (last - 1, y_hi_of, 0),
                (last - 1, y_hi_of, 1), (last - 2, o_out, 1), (last, guess_reciprocal), (last - 2, o_out, 2),
                (last - 2, o_out, 3), (last, spread_some), (last - 1, o_out, 0), (last - 1, o_out, 1),
                (last, evacuate_y, 0), (last, evacuate_y, 1), (last, copy_some_y), (last, y_hi_of, 0),
                (last, y_hi_of, 1), (last - 1, o_out, 2), (last - 1, o_out, 3), (last, o_out, 0), (last, o_out, 1),
                (last, o_out, 2), (last, o_out, 3)]
            for c, step, *args in act_head + [s for i in range(DEPTH + 1, last) for s in act_steps(i)] + act_tail:
                step(c, *args)

        @block.vector
        def _(dve):
            def lo_part(l, c, h, out, src, hi, made, raised):
                b = c // PER_BATCH
                dve.wait_ge(made, 2 * c + h + 1)
                for k in range(h * KB // 2, (h + 1) * KB // 2):
                    v = dve.scalar_tensor_tensor(out=out[:, k], in0=src[:, k], scalar=style[l][:, k, b:b + 1],
                                                 in1=hi[:, k], op0=ALU.mult, op1=ALU.subtract)
                v.then_inc(raised, 1)

            def x_lo_of(c, h):
                lo_part(L0, c, h, x_lo, x_sb[:, c % 2], x_hi, a_xhi, v_xlo)

            def x1_lo_of(c, h):
                lo_part(K, c, h, x1_lo, x1_sb[:, c % NX1], x1_hi, a_x1hi, v_x1lo)

            def y_lo_of(c, h):
                lo_part(O, c, h, y_lo[:, c % 2], yr_sb, y_hi[:, c % 2], a_yhi, v_ylo)

            def style_of(l):
                dve.wait_ge(pe_style, l + 1)
                dve.scalar_tensor_tensor(
                    out=style[l][:], in0=y_ps[:, 0, l * KB * B:(l + 1) * KB * B].rearrange("p (k b) -> p k b", b=B),
                    scalar=GAIN[l], in1=affb_sb[l][:].unsqueeze(2).to_broadcast([P, KB, B]),
                    op0=ALU.mult, op1=ALU.add).then_inc(v_style, 1)
                dve.wait_ge(v_style, l + 1)
                dve.tensor_tensor(style_sq[l][:], style[l][:], style[l][:], ALU.mult).then_inc(v_ssq, 1)

            def weights_lo(l, h):
                ks = slice(h * KB // 2, (h + 1) * KB // 2)
                dve.wait_ge(a_whi, 2 * l + h + 1)
                dve.tensor_tensor(w_lo[l][:, ks], w_raw[l][:, ks], w_hi[l][:, ks], ALU.subtract).then_inc(v_wlo, 1)

            def demod_of(l):
                dve.wait_ge(a_norm, l + 1)
                dve.reciprocal(demod[l][:], norm[l][:]).then_inc(v_demod, 1)

            dve.wait_ge(ld_first, DMA * FIRST)
            style_of(L0)
            x_lo_of(0, 0)
            weights_lo(L0, 0)
            x_lo_of(0, 1)
            weights_lo(L0, 1)
            weights_lo(K, 0)
            weights_lo(K, 1)
            demod_of(L0)
            dve.wait_ge(ld_small, DMA * SMALL)
            dve.tensor_copy(k_rhs[:, HEADS:NC, :], eye[:].unsqueeze(2).to_broadcast([P, HD, TB])).then_inc(v_eye, 1)

            def copy_y(c, h):
                if h and c >= SHARED_Y:
                    return
                dve.wait_ge(a_y, NPB * (c + 1))
                if c:
                    dve.wait_ge(a_yhi, 2 * c)
                    dve.wait_ge(v_ylo, 2 * c)
                for j in range(h * HR // 2, (h + 1) * HR // 2):
                    v = heads_to_partitions(dve.tensor_copy, j)
                if h or c >= SHARED_Y:
                    v.then_inc(v_yr, 1)

            def copy_k(c):
                dve.wait_ge(a_lin, done(K, c, KB - 1))
                if c:
                    dve.wait_ge(pe_s, SU * c)
                for part in range(HR, 2 * HR):
                    kx_to_block(dve.tensor_copy, c, part).then_inc(v_krhs, 1)

            def make_x1(c, h):
                x1h = x1_sb[:, c % NX1, h * half:(h + 1) * half]
                dve.wait_ge(a_lin, done(L0, c, (h + 1) * half - 1))
                dve.tensor_scalar(x1h, x1h, CLAMP, -CLAMP, ALU.min, ALU.max).then_inc(v_clip, 1)
                dve.wait_ge(v_clip, 2 * c + h + 1)
                dve.tensor_tensor(x1h, x1h, x_sb[:, c % 2, h * half:(h + 1) * half], ALU.add).then_inc(v_x1, 1)

            def maxima(c):
                dve.wait_ge(a_sv, SU * (c + 1))
                dve.tensor_reduce(out=mx[:], in_=sv_sb[:, c % 2, :, 0:HEADS], axis=AX_X,
                                  op=ALU.max).then_inc(v_max, 1)
                dve.wait_ge(v_max, c + 1)
                dve.tensor_copy(mx_hi[:], mx[:]).then_inc(v_mhi, 1)
                dve.wait_ge(v_mhi, c + 1)
                dve.tensor_tensor(mx_lo[:], mx[:], mx_hi[:], ALU.subtract).then_inc(v_mlo, 1)
                dve.wait_ge(v_mlo, c + 1)
                for src, dst in ((mx_hi, md_hi), (mx_lo, md_lo)):
                    v = dve.tensor_tensor(dst[:], src[:].unsqueeze(2).to_broadcast([P, NG, HEADS]),
                                          diag[:].unsqueeze(1).to_broadcast([P, NG, HEADS]), ALU.mult)
                v.then_inc(v_diag, 1)

            def finish(c, h):
                oh = o_sb[:, c % 2, h * half:(h + 1) * half]
                dve.wait_ge(a_lin, done(O, c, (h + 1) * half - 1))
                dve.tensor_tensor(oh, oh, x1_sb[:, c % NX1, h * half:(h + 1) * half], ALU.add).then_inc(v_out, 1)

            half = KB // 2
            def refine_reciprocal(c):
                dve.wait_ge(a_rcp, c + 1)
                dve.tensor_tensor(err[:], rcp[:], cd_ps[:, :].rearrange("p (g h) -> p g h", h=HEADS),
                                  ALU.mult).then_inc(v_err, 1)
                dve.wait_ge(v_err, c + 1)
                dve.scalar_tensor_tensor(out=rcp[:], in0=err[:], scalar=2.0, in1=rcp[:],
                                         op0=ALU.subtract, op1=ALU.mult).then_inc(v_rcp, 1)
                dve.wait_ge(v_rcp, c + 1)
                dve.scalar_tensor_tensor(out=prob[:], in0=rcp[:], scalar=-1.0, in1=ex[:],
                                         op0=ALU.mult, op1=ALU.mult).then_inc(v_prob, 1)

            def spread_probabilities(c):
                dve.wait_ge(v_prob, c + 1)
                dve.wait_ge(pe_pv, NPB * c)
                for t in range(TG if c < SHARED_P else TG // 2):
                    v = dve.tensor_scalar(p_bd[:, :, t, :], prob[:], tok_mask[:, t:t + 1], None, ALU.mult)
                v.then_inc(v_pbd, 1)

            def subtract_maxima(c):
                dve.wait_ge(pe_c, c + 1)
                dve.tensor_tensor(ex[:], sv_sb[:, c % 2, :, 0:HEADS],
                                  cd_ps[:, :].rearrange("p (g h) -> p g h", h=HEADS),
                                  ALU.subtract).then_inc(v_sub, 1)

            def split_exponentials(c):
                dve.wait_ge(a_exp, c + 1)
                dve.tensor_copy(ex_hi[:], ex[:]).then_inc(v_ehi, 1)
                dve.wait_ge(v_ehi, c + 1)
                dve.tensor_tensor(ex_lo[:], ex[:], ex_hi[:], ALU.subtract).then_inc(v_elo, 1)

            def dve_steps(i):
                c0, c1, c2, c3, c4 = range(i, i - 5, -1)
                return [
                    (c2, subtract_maxima), (c0, make_x1, 0), (c2, split_exponentials), (c0, make_x1, 1),
                    (c0, x1_lo_of, 0), (c3, copy_y, 0), (c0, x1_lo_of, 1),
                    (c2, refine_reciprocal), (c4, finish, 0), (c2, spread_probabilities), (c4, finish, 1),
                    (c3, copy_y, 1), (i + 1, x_lo_of, 0), (i + 1, x_lo_of, 1),
                    (c3, y_lo_of, 0), (c3, y_lo_of, 1), (c1, maxima)]

            dve_head = [
                (1, x_lo_of, 0), (1, x_lo_of, 1), (K, style_of), (0, make_x1, 0), (0, make_x1, 1), (O, style_of),
                (0, x1_lo_of, 0), (0, x1_lo_of, 1), (1, make_x1, 0), (K, demod_of), (O, weights_lo, 0),
                (O, weights_lo, 1), (2, x_lo_of, 0), (O, demod_of), (1, make_x1, 1), (2, x_lo_of, 1),
                (1, x1_lo_of, 0), (0, copy_k), (1, x1_lo_of, 1), (2, make_x1, 0), (2, make_x1, 1), (2, x1_lo_of, 0),
                (3, x_lo_of, 0), (3, x_lo_of, 1), (1, copy_k), (0, maxima), (0, subtract_maxima),
                (0, split_exponentials), (2, x1_lo_of, 1), (4, x_lo_of, 0), (3, make_x1, 0), (3, make_x1, 1),
                (0, refine_reciprocal), (4, x_lo_of, 1), (0, spread_probabilities), (3, x1_lo_of, 0),
                (3, x1_lo_of, 1), (1, maxima), (2, copy_k), (1, subtract_maxima), (1, split_exponentials),
                (0, copy_y, 0), (0, copy_y, 1), (4, make_x1, 0), (1, refine_reciprocal), (1, spread_probabilities),
                (0, y_lo_of, 0), (0, y_lo_of, 1), (2, maxima), (2, subtract_maxima), (4, make_x1, 1),
                (2, split_exponentials), (1, copy_y, 0), (4, x1_lo_of, 0), (4, x1_lo_of, 1), (1, copy_y, 1),
                (2, refine_reciprocal), (2, spread_probabilities), (0, finish, 0), (0, finish, 1), (5, x_lo_of, 0),
                (5, x_lo_of, 1), (1, y_lo_of, 0), (1, y_lo_of, 1), (3, maxima)]
            dve_tail = [
                (last - 2, subtract_maxima), (last, make_x1, 0), (last - 2, split_exponentials), (last, make_x1, 1),
                (last, x1_lo_of, 0), (last, x1_lo_of, 1), (last - 3, copy_y, 0), (last - 3, copy_y, 1),
                (last - 4, finish, 0), (last - 2, refine_reciprocal), (last - 2, spread_probabilities),
                (last - 3, y_lo_of, 0), (last, copy_k), (last - 1, maxima), (last - 3, y_lo_of, 1),
                (last - 1, subtract_maxima), (last - 2, copy_y, 0), (last - 1, split_exponentials),
                (last - 4, finish, 1), (last - 3, finish, 0), (last - 2, y_lo_of, 0), (last - 1, refine_reciprocal),
                (last - 2, y_lo_of, 1), (last - 1, spread_probabilities), (last, maxima), (last - 3, finish, 1),
                (last, subtract_maxima), (last - 1, copy_y, 0), (last, split_exponentials), (last - 1, y_lo_of, 0),
                (last - 1, y_lo_of, 1), (last, refine_reciprocal), (last, spread_probabilities), (last, copy_y, 0),
                (last - 2, finish, 0), (last - 2, finish, 1), (last - 1, finish, 0), (last, y_lo_of, 0),
                (last, y_lo_of, 1), (last - 1, finish, 1), (last, finish, 0), (last, finish, 1)]
            for c, step, *args in dve_head + [s for i in range(DEPTH + 1, last) for s in dve_steps(i)] + dve_tail:
                step(c, *args)


FIRST, SMALL = 3, 11

_LAYERS = (("L0_cond_weight", "L0_cond_affine_w", "L0_cond_affine_b", "L0_cond_bias"),
           ("L1_cond_k_w", "L1_cond_k_aff_w", "L1_cond_k_aff_b", "L1_cond_k_b"),
           ("L1_cond_o_w", "L1_cond_o_aff_w", "L1_cond_o_aff_b", "L1_cond_o_b"))


def kernel(**inputs):
    import numpy as np
    import concourse.bacc as bacc
    from concourse.bass_utils import run_bass_kernel_spmd

    x = np.asarray(inputs["x"])
    B, L, F = x.shape
    part = np.arange(P)
    cols = lambda v: np.ascontiguousarray(np.asarray(v).reshape(F // P, P).T)
    turned = lambda a: np.ascontiguousarray(np.asarray(a).T)
    arrays = {"xT": turned(x.reshape(B * L, F)), "condT": turned(inputs["cond_512"])}
    for l, (w, aw, ab, b) in enumerate(_LAYERS):
        arrays[f"wT{l}"], arrays[f"affT{l}"] = turned(inputs[w]), turned(inputs[aw])
        arrays[f"aff_b{l}"], arrays[f"lin_b{l}"] = cols(inputs[ab]), cols(inputs[b])
    HD = F // HEADS
    arrays["block_ones"] = (part[:, None] // HEADS == part[None, :] // HEADS).astype(np.float32)
    arrays["token_mask"] = (part[:, None] // HEADS == np.arange(P // HEADS)[None, :]).astype(np.float32)
    arrays["head_diag"] = (part[:, None] % HEADS == np.arange(HEADS)[None, :]).astype(np.float32)
    arrays["dim_eye"] = (part[:, None] % HD == np.arange(HD)[None, :]).astype(np.float32)

    nc = bacc.Bacc("TRN2", target_bir_lowering=False, num_devices=1)
    d = {n: nc.dram_tensor(n, a.shape, mybir.dt.from_np(a.dtype), kind="ExternalInput").ap() for n, a in arrays.items()}
    outT = nc.dram_tensor("outT", (F, B * L), F32, kind="ExternalOutput").ap()
    three = lambda n: [d[f"{n}{l}"] for l in range(3)]
    build(nc, d["xT"], d["condT"], three("wT"), three("affT"), three("aff_b"), three("lin_b"),
          d["block_ones"], d["token_mask"], d["head_diag"], d["dim_eye"], outT)
    r = run_bass_kernel_spmd(nc, [arrays], core_ids=[0])
    return np.ascontiguousarray(r.results[0]["outT"].T).reshape(B, L, F)
```
